# Optimizing a Trainium2 kernel written in Bass

```python
import numpy as np
import jax
import jax.numpy as jnp

def _softmax(x, axis=-1):
    return jax.nn.softmax(x, axis=axis)

def _gelu(x):
    return jax.nn.gelu(x, approximate=True)

def _silu(x):
    return jax.nn.silu(x)

def _sigmoid(x):
    return jax.nn.sigmoid(x)

def _layernorm(x, axis=-1, eps=1e-05):
    m = jnp.mean(x, axis=axis, keepdims=True)
    v = jnp.var(x, axis=axis, keepdims=True)
    return (x - m) / jnp.sqrt(v + eps)

def _scatter_add(tgt, idx, src, axis=0):
    return tgt.at[idx].add(src)

def _segment_sum(src, seg, n):
    return jax.ops.segment_sum(src, seg, n)
kernel_name = 'mk_adaln_ffn_d2_seqx_r8_b6a31a'

def setup_inputs(seed: int=0):
    np.random.seed(seed)
    _w = jnp.asarray

    def _rec_inputs():
        import jax
        import jax.numpy as jnp
        _rk = jax.random.key(seed)
        x = -0.000125 + 0.9999 * jax.random.normal(jax.random.fold_in(_rk, 1), (8, 128, 128), jnp.float32)
        _lenS = 128 - jax.random.randint(jax.random.fold_in(_rk, 7), (8,), 0, max(1, 128 // 4) + 1, jnp.int32)
        _lenS2 = 128 - jax.random.randint(jax.random.fold_in(_rk, 8), (8,), 0, max(1, 128 // 4) + 1, jnp.int32)
        cond_1024 = -0.00493535 + 1.00056 * jax.random.normal(jax.random.fold_in(_rk, 11), (8, 128), jnp.float32)
        return (x, cond_1024)
    x, cond_1024 = _rec_inputs()

    def _L0_cond_setup():
        import jax, jax.numpy as jnp
        import numpy as np
        import math
        N, T, D, H = (64, 64, 128, 128)
        key = jax.random.key(seed)
        k1, k2, k3, k4 = jax.random.split(key, 4)
        x = jax.random.normal(k1, (N, T, D), dtype=jnp.float32)
        h0 = jax.random.normal(k2, (N, H), dtype=jnp.float32)
        Wx = jax.random.normal(k3, (D, H), dtype=jnp.float32) / math.sqrt(D)
        Wh = jax.random.normal(k4, (H, H), dtype=jnp.float32) / math.sqrt(H)
        b = jnp.zeros((H,), dtype=jnp.float32)
        return {'x': x, 'h0': h0, 'Wx': Wx, 'Wh': Wh, 'b': b}
    _L0_cond_all = _L0_cond_setup()
    _L0_cond_in = {k: v for k, v in _L0_cond_all.items() if k in ('Wx', 'Wh', 'b')}
    del _L0_cond_all

    def _L0_ffn_setup():
        import jax, jax.numpy as jnp
        import numpy as np
        TOPK = 4
        N_GROUPS = 4
        TOPK_GROUPS = 2
        ROUTE_SCALE = 2.5

        def _gate(x2, Wg):
            T = x2.shape[0]
            E = Wg.shape[0]
            scores = x2 @ Wg.T
            s = jax.nn.sigmoid(scores)
            g = s.reshape(T, N_GROUPS, E // N_GROUPS)
            group_scores = g.max(axis=-1)
            _, gidx = jax.lax.top_k(group_scores, TOPK_GROUPS)
            group_mask = jnp.any(jax.nn.one_hot(gidx, N_GROUPS, dtype=jnp.bool_), axis=1)
            masked = jnp.where(group_mask[:, :, None], g, -jnp.inf).reshape(T, E)
            _, idx = jax.lax.top_k(masked, TOPK)
            w = jnp.take_along_axis(s, idx, axis=1)
            w = w / jnp.sum(w, axis=-1, keepdims=True)
            w = w * ROUTE_SCALE
            return (w.astype(x2.dtype), idx)
        key = jax.random.key(seed)
        ks = jax.random.split(key, 6)
        B, S, D, I, E = (2, 256, 128, 128, 16)
        scale = 0.02
        return {'x': jax.random.normal(ks[0], (B, S, D), dtype=jnp.float32), 'Wg': jax.random.normal(ks[1], (E, D), dtype=jnp.float32) * scale, 'W1': jax.random.normal(ks[2], (E, I, D), dtype=jnp.float32) * scale, 'b1': jnp.zeros((E, I), dtype=jnp.float32), 'W2': jax.random.normal(ks[3], (E, D, I), dtype=jnp.float32) * scale, 'b2': jnp.zeros((E, D), dtype=jnp.float32), 'W3': jax.random.normal(ks[4], (E, I, D), dtype=jnp.float32) * scale, 'b3': jnp.zeros((E, I), dtype=jnp.float32)}
    _L0_ffn_all = _L0_ffn_setup()
    _L0_ffn_in = {k: v for k, v in _L0_ffn_all.items() if k in ('Wg', 'W1', 'b1', 'W2', 'b2', 'W3', 'b3')}
    del _L0_ffn_all

    def _L1_cond_setup():
        import jax, jax.numpy as jnp
        import numpy as np
        IN_FEATURES = 128
        OUT_FEATURES = 128
        BATCH = 32
        SEQ = 128
        EPS = 1e-08
        key = jax.random.key(seed)
        k1, k2, k3 = jax.random.split(key, 3)
        Efou = jax.random.normal(k1, (BATCH, SEQ, IN_FEATURES), dtype=jnp.float32)
        y = jax.random.normal(k2, (BATCH, IN_FEATURES), dtype=jnp.float32)
        weight = jax.random.normal(k3, (IN_FEATURES, OUT_FEATURES), dtype=jnp.float32)
        return {'Efou': Efou, 'y': y, 'weight': weight}
    _L1_cond_all = _L1_cond_setup()
    _L1_cond_in = {k: v for k, v in _L1_cond_all.items() if k in ('weight',)}
    del _L1_cond_all

    def _L1_ffn_setup():
        import jax, jax.numpy as jnp
        import numpy as np
        QB = 127.0
        EPS = 1e-05

        def _ste(x, q):
            return x + jax.lax.stop_gradient(q - x)

        def bitlinear(x, W, b):
            w_scale = jnp.clip(jnp.mean(jnp.abs(W)), EPS, None)
            Wq = _ste(W, jnp.clip(jnp.round(W / w_scale), -1.0, 1.0) * w_scale)
            x_scale = jnp.clip(jnp.max(jnp.abs(x), axis=-1, keepdims=True), EPS, None)
            xq = _ste(x, jnp.clip(jnp.round(x * (QB / x_scale)), -QB - 1.0, QB) * (x_scale / QB))
            return jnp.einsum('bnd,hd->bnh', xq, Wq) + b
        key = jax.random.key(seed)
        k0, k1, k2 = jax.random.split(key, 3)
        B, N, D = (8, 512, 128)
        H = int(D * 4.0)
        x = jax.random.normal(k0, (B, N, D), dtype=jnp.float32)
        W1 = jax.random.normal(k1, (H, D), dtype=jnp.float32) * 0.02
        b1 = jnp.zeros((H,), dtype=jnp.float32)
        W2 = jax.random.normal(k2, (D, H), dtype=jnp.float32) * 0.02
        b2 = jnp.zeros((D,), dtype=jnp.float32)
        return {'x': x, 'W1': W1, 'b1': b1, 'W2': W2, 'b2': b2}
    _L1_ffn_all = _L1_ffn_setup()
    _L1_ffn_in = {k: v for k, v in _L1_ffn_all.items() if k in ('W1', 'b1', 'W2', 'b2')}
    del _L1_ffn_all
    return {'x': x, 'cond_1024': cond_1024, 'L0_cond_Wx': _L0_cond_in['Wx'], 'L0_cond_Wh': _L0_cond_in['Wh'], 'L0_cond_b': _L0_cond_in['b'], 'L0_ffn_Wg': _L0_ffn_in['Wg'], 'L0_ffn_W1': _L0_ffn_in['W1'], 'L0_ffn_b1': _L0_ffn_in['b1'], 'L0_ffn_W2': _L0_ffn_in['W2'], 'L0_ffn_b2': _L0_ffn_in['b2'], 'L0_ffn_W3': _L0_ffn_in['W3'], 'L0_ffn_b3': _L0_ffn_in['b3'], 'L1_cond_weight': _L1_cond_in['weight'], 'L1_ffn_W1': _L1_ffn_in['W1'], 'L1_ffn_b1': _L1_ffn_in['b1'], 'L1_ffn_W2': _L1_ffn_in['W2'], 'L1_ffn_b2': _L1_ffn_in['b2']}

def reference(x, cond_1024, L0_cond_Wx, L0_cond_Wh, L0_cond_b, L0_ffn_Wg, L0_ffn_W1, L0_ffn_b1, L0_ffn_W2, L0_ffn_b2, L0_ffn_W3, L0_ffn_b3, L1_cond_weight, L1_ffn_W1, L1_ffn_b1, L1_ffn_W2, L1_ffn_b2):
    import jax
    import jax.numpy as jnp

    def _L0_cond_ref(x, h0, Wx, Wh, b):
        import jax, jax.numpy as jnp
        import numpy as np
        import math
        N, T, D, H = (64, 64, 128, 128)
        xW = jnp.einsum('ntd,dh->nth', x, Wx) + b

        def step(prev_h, xw_t):
            next_h = jnp.tanh(prev_h @ Wh + xw_t)
            return (next_h, next_h)
        _, hs = jax.lax.scan(step, h0, jnp.swapaxes(xW, 0, 1))
        return jnp.swapaxes(hs, 0, 1)

    def _L0_ffn_ref(x, Wg, W1, b1, W2, b2, W3, b3):
        import jax, jax.numpy as jnp
        import numpy as np
        TOPK = 4
        N_GROUPS = 4
        TOPK_GROUPS = 2
        ROUTE_SCALE = 2.5

        def _gate(x2, Wg):
            T = x2.shape[0]
            E = Wg.shape[0]
            scores = x2 @ Wg.T
            s = jax.nn.sigmoid(scores)
            g = s.reshape(T, N_GROUPS, E // N_GROUPS)
            group_scores = g.max(axis=-1)
            _, gidx = jax.lax.top_k(group_scores, TOPK_GROUPS)
            group_mask = jnp.any(jax.nn.one_hot(gidx, N_GROUPS, dtype=jnp.bool_), axis=1)
            masked = jnp.where(group_mask[:, :, None], g, -jnp.inf).reshape(T, E)
            _, idx = jax.lax.top_k(masked, TOPK)
            w = jnp.take_along_axis(s, idx, axis=1)
            w = w / jnp.sum(w, axis=-1, keepdims=True)
            w = w * ROUTE_SCALE
            return (w.astype(x2.dtype), idx)
        shape = x.shape
        D = shape[-1]
        x2 = x.reshape(-1, D)
        weights, indices = _gate(x2, Wg)
        E = Wg.shape[0]
        y = jnp.zeros_like(x2)
        for e in range(E):
            we = jnp.sum(weights * (indices == e), axis=-1)
            h = jax.nn.silu(x2 @ W1[e].T + b1[e]) * (x2 @ W3[e].T + b3[e])
            y = y + (h @ W2[e].T + b2[e]) * we[:, None]
        return y.reshape(shape)

    def _L1_cond_ref(Efou, y, weight):
        import jax, jax.numpy as jnp
        import numpy as np
        IN_FEATURES = 128
        OUT_FEATURES = 128
        BATCH = 32
        SEQ = 128
        EPS = 1e-08
        scale = 1.0 / np.sqrt(np.float32(weight.shape[0]))
        ys = y * scale
        d = jax.lax.rsqrt(jnp.einsum('bi,io->bo', ys * ys, weight * weight) + EPS)
        out = jnp.einsum('bsi,io->bso', Efou * ys[:, None, :], weight) * d[:, None, :]
        return out

    def _L1_ffn_ref(x, W1, b1, W2, b2):
        import jax, jax.numpy as jnp
        import numpy as np
        QB = 127.0
        EPS = 1e-05

        def _ste(x, q):
            return x + jax.lax.stop_gradient(q - x)

        def bitlinear(x, W, b):
            w_scale = jnp.clip(jnp.mean(jnp.abs(W)), EPS, None)
            Wq = _ste(W, jnp.clip(jnp.round(W / w_scale), -1.0, 1.0) * w_scale)
            x_scale = jnp.clip(jnp.max(jnp.abs(x), axis=-1, keepdims=True), EPS, None)
            xq = _ste(x, jnp.clip(jnp.round(x * (QB / x_scale)), -QB - 1.0, QB) * (x_scale / QB))
            return jnp.einsum('bnd,hd->bnh', xq, Wq) + b
        h = bitlinear(x, W1, b1)
        h = jax.nn.gelu(h, approximate=False)
        return bitlinear(h, W2, b2)
    x = x + _L0_ffn_ref(_L0_cond_ref(x, cond_1024, L0_cond_Wx, L0_cond_Wh, L0_cond_b), L0_ffn_Wg, L0_ffn_W1, L0_ffn_b1, L0_ffn_W2, L0_ffn_b2, L0_ffn_W3, L0_ffn_b3)
    x = x + _L1_ffn_ref(_L1_cond_ref(x, cond_1024, L1_cond_weight), L1_ffn_W1, L1_ffn_b1, L1_ffn_W2, L1_ffn_b2)
    return x

_drawn_inputs = setup_inputs


def setup_inputs(seed=0):
    import zlib

    import numpy as np

    out = dict(_drawn_inputs(seed))
    spreads = {'L0_cond_b': (0.0, 0.1),
     'L0_ffn_b1': (0.0, 0.8),
     'L0_ffn_b2': (0.0, 0.1),
     'L0_ffn_b3': (0.0, 0.8),
     'L1_ffn_b1': (0.0, 1.463),
     'L1_ffn_b2': (0.0, 0.1)}
    factors = {'L0_ffn_W1': 8.0, 'L0_ffn_W2': 8.0, 'L0_ffn_W3': 8.0}
    for name, (base, spread) in spreads.items():
        noise = np.random.default_rng([zlib.crc32(name.encode()), seed]).standard_normal(out[name].shape)
        drawn = base * np.exp(spread * noise) if base else spread * noise
        out[name] = jnp.asarray(drawn.astype(out[name].dtype))
    for name, factor in factors.items():
        out[name] = (out[name] * factor).astype(out[name].dtype)
    return out
```

```python
from contextlib import ExitStack

import concourse.bass as bass
from concourse import mybir

ALU = mybir.AluOpType
ACT = mybir.ActivationFunctionType
AX_X = mybir.AxisListType.X
F32 = mybir.dt.float32
F32R = mybir.dt.float32r
BF16 = mybir.dt.bfloat16

P = 128
BATCH = 8
STEPS = 128
TOKENS = BATCH * STEPS
TILES = TOKENS // P
STEPS_PER_TILE = P // BATCH
BANK = 512
EXPERTS = 16
GROUPS = 4
TOP_GROUPS = 2
TOP_EXPERTS = 4
ROUTE_SCALE = 2.5
QB = 127.0
HIDDEN = 512
HB = HIDDEN // P
MAGIC = 1.5 * 2.0 ** 23
E_CONST = 2.718281828459045

CHUNKS = [(0, 1), (1, 1), (2, 2), (4, 2), (6, 2)]
JOBS = len(CHUNKS) * EXPERTS
H_RING = 24
W_LAG = 13
Y_LAG = W_LAG + 2
QUOTA = 0.43
GATE_STEPS = 14


def chunk_of(j):
    return CHUNKS[j // EXPERTS]


def build_schedule():
    pieces = []
    pos_l1 = {}

    def at(k, kind, n):
        pos_l1.setdefault(k, []).append((kind, n))

    for k in range(JOBS + Y_LAG):
        if k < JOBS:
            pieces += [("A", k), ("B", k)]
        if 0 <= k - W_LAG < JOBS:
            pieces.append(("W", k - W_LAG))
        j = k - Y_LAG
        if j >= 0:
            pieces.append(("Y", j))
            if j % EXPERTS == EXPERTS - 1:
                c = j // EXPERTS
                pieces.append(("FIN", c))
                for n in range(CHUNKS[c][1]):
                    i = CHUNKS[c][0] + n
                    for d, kind in enumerate(("X", "Q", "HP", "GELU", "Q2", "T2", "OUT")):
                        at(k + 1 + d + 3 * n, kind, i)
        for entry in pos_l1.pop(k, []):
            pieces.append(entry)
    for k in sorted(pos_l1):
        pieces += pos_l1[k]

    schedule, ready_chunks, ready_weights = [], set(), set()
    credit, nxt = 0.0, 0

    def cost(kind, n):
        if kind in "AB":
            return 0.213 if chunk_of(n)[1] == 1 else 0.321
        if kind == "Y":
            return 0.213 * chunk_of(n)[1]
        return {"X": 0.32, "HP": 0.21, "T2": 0.2, "OUT": 0.2}.get(kind, 0.05)

    def open_now(kind, n, t):
        if kind == "A":
            return n // EXPERTS in ready_chunks
        if kind == "W":
            return n // EXPERTS in ready_weights
        if kind == "X":
            return t > STEPS // 2
        return True

    def weights(i):
        schedule.append(("WT", i))
        for c, (first, n) in enumerate(CHUNKS):
            if first + n - 1 == i:
                schedule.append(("WB", c))
                ready_weights.add(c)

    def tile_done(i):
        schedule.append(("SCORES", i))
        for c, (first, n) in enumerate(CHUNKS):
            if first + n - 1 == i:
                if n > 1:
                    schedule.append(("SPLIT", c))
                ready_chunks.add(c)

    for t in range(STEPS):
        schedule.append(("RNN", t))
        if t and t % STEPS_PER_TILE == 0:
            tile_done(t // STEPS_PER_TILE - 1)
        since = t - GATE_STEPS + 6
        if since > 0 and since % STEPS_PER_TILE == 0:
            schedule.append(("GATE", since // STEPS_PER_TILE - 1))
        since = t - GATE_STEPS
        if since > 0 and since % STEPS_PER_TILE == 0:
            weights(since // STEPS_PER_TILE - 1)
        credit = min(credit + QUOTA, 2 * QUOTA)
        while nxt < len(pieces) and credit > 0 and open_now(*pieces[nxt], t):
            credit -= cost(*pieces[nxt])
            schedule.append(pieces[nxt])
            nxt += 1
    tile_done(TILES - 1)
    done = [i for kind, i in schedule if kind == "WT"]
    gates = [i for kind, i in schedule if kind == "GATE"]
    spent = 0.0
    owed = [(2.0 if i < TILES - 1 else 4.5, "GATE", i) for i in range(TILES) if i not in gates]
    owed += [(4.0 if i < TILES - 1 else 8.0, "WT", i) for i in range(TILES) if i not in done]
    owed.sort()
    while nxt < len(pieces) or owed:
        if owed and (spent >= owed[0][0] or nxt == len(pieces) or not open_now(*pieces[nxt], STEPS)):
            _, kind, i = owed.pop(0)
            if kind == "WT":
                weights(i)
            else:
                schedule.append((kind, i))
            continue
        schedule.append(pieces[nxt])
        spent += cost(*pieces[nxt])
        nxt += 1
    return schedule


SCHEDULE = build_schedule()

M, R0, R1 = range(3)


def bank_of(kind, i):
    if kind in ("SCORES", "WT", "Q"):
        return M
    if kind in ("X", "HP"):
        return R1 if i == TILES - 1 else R0
    return R1 if i == TILES - 1 else M


def bank_uses():
    count, place = [0, 0, 0], {}
    for kind, i in SCHEDULE:
        if kind in ("SCORES", "WT", "X", "Q", "HP", "T2", "OUT"):
            b = bank_of(kind, i)
            place[(kind, i)] = (b, count[b])
            count[b] += 1
    return place


USES = bank_uses()


def adaln_ffn(nc, x_nat, xT, h0T, Wx, Wh, bh, WgT, W1T, W3T, W2T, b1T, b3T, b2e,
              condT, Wc, F1T, F2T, fb1, fb2, we_dram, out):
    with ExitStack() as ctx:
        def sb(name, shape, dt=F32):
            return ctx.enter_context(nc.sbuf_tensor(name, shape, dt))

        def psum(name):
            return ctx.enter_context(nc.psum_tensor(name, [P, BANK], F32))

        def sem(name):
            return ctx.enter_context(nc.semaphore(name))

        xT_sb = sb("xT_sb", [P, TOKENS])
        xn_sb = None
        h0_sb = sb("h0_sb", [P, BATCH])
        wx_sb, wh_sb = sb("wx_sb", [P, P]), sb("wh_sb", [P, P])
        bh_sb = sb("bh_sb", [1, P])
        ones_row = sb("ones_row", [1, BANK])
        hs = sb("hs", [P, TOKENS])
        hs_hi, hs_lo = sb("hs_hi", [P, TOKENS], F32R), sb("hs_lo", [P, TOKENS], F32R)
        w1_sb, w3_sb = sb("w1_sb", [P, EXPERTS * P]), sb("w3_sb", [P, EXPERTS * P])
        w2_sb = sb("w2_sb", [P, EXPERTS * P])
        w1_hi, w1_lo = sb("w1_hi", [P, EXPERTS * P], F32R), sb("w1_lo", [P, EXPERTS * P], F32R)
        w3_hi, w3_lo = sb("w3_hi", [P, EXPERTS * P], F32R), sb("w3_lo", [P, EXPERTS * P], F32R)
        b1_sb, b1_half, b3_sb = sb("b1_sb", [P, EXPERTS]), sb("b1_half", [P, EXPERTS]), sb("b3_sb", [P, EXPERTS])
        b2e_sb = sb("b2e_sb", [EXPERTS, P])
        wg_sb = sb("wg_sb", [P, EXPERTS])
        gate_t = sb("gate_t", [P, 4, 256])
        hid = sb("hid", [P, H_RING, 256])
        we_bc = sb("we_bc", [P, 2, EXPERTS, 256])
        weT = sb("weT", [EXPERTS, TOKENS])
        e_const = sb("e_const", [P, EXPERTS])
        neg_scores, exp_neg = sb("neg_scores", [P, TILES, EXPERTS]), sb("exp_neg", [P, TILES, EXPERTS])
        s_gate = sb("s_gate", [P, EXPERTS])
        gmax = sb("gmax", [P, 8])
        top8 = sb("top8", [P, 8])
        above, equal, before = (sb(n, [P, EXPERTS]) for n in ("above", "equal", "before"))
        n_above = sb("n_above", [P, 1])
        fits = sb("fits", [P, EXPERTS])
        g_sel, e_sel = sb("g_sel", [P, GROUPS]), sb("e_sel", [P, EXPERTS])
        masked = sb("masked", [P, EXPERTS])
        zeros16 = sb("zeros16", [P, EXPERTS])
        w_raw, w_sum, w_inv = sb("w_raw", [P, EXPERTS]), sb("w_sum", [P, 1]), sb("w_inv", [P, 1])
        we = sb("we", [P, TILES, EXPERTS])
        x1T, zT = sb("x1T", [P, TOKENS]), sb("zT", [P, TOKENS])
        cond_sb, ysT, ys2 = sb("cond_sb", [P, BATCH]), sb("ysT", [P, BATCH]), sb("ys2", [P, BATCH])
        wc_sb, wc2 = sb("wc_sb", [P, P]), sb("wc2", [P, P])
        neg_half, d_sum, dT = sb("neg_half", [P, BATCH]), sb("d_sum", [P, BATCH]), sb("dT", [P, BATCH])
        dT_rep = sb("dT_rep", [P, P])
        demod = sb("demod", [P, P])
        f1_sb, f2_sb = sb("f1_sb", [P, HIDDEN]), sb("f2_sb", [P, HIDDEN])
        f1_q, f2_q = sb("f1_q", [P, HIDDEN], BF16), sb("f2_q", [P, HB, P], BF16)
        f_abs, f_scale, f_inv, f_scale_q = (sb(n, [P, 2]) for n in ("f_abs", "f_scale", "f_inv", "f_scale_q"))
        fb1_bc, fb2_bc = sb("fb1_bc", [P, HIDDEN]), sb("fb2_bc", [P, P])
        ident, ident_bf, ones_sq = sb("ident", [P, P]), sb("ident_bf", [P, P], BF16), sb("ones_sq", [P, P])
        x1b = sb("x1b", [P, TILES, P])
        o_sb, q_f = sb("o_sb", [P, P]), sb("q_f", [P, P])
        q_bf, qT = sb("q_bf", [P, 2, P], BF16), sb("qT", [P, 2, P], BF16)
        amax, xs, xinv = (sb(n, [P, 2 * TILES]) for n in ("amax", "xs", "xinv"))
        x127, deq = sb("x127", [P, 2 * TILES]), sb("deq", [P, 2 * TILES])
        hp = sb("hp", [P, 4, HIDDEN])
        q2_f, q2_bf, q2T = sb("q2_f", [P, HIDDEN]), sb("q2_bf", [P, 2, HIDDEN], BF16), sb("q2T", [P, 2, HIDDEN], BF16)
        out_sb = sb("out_sb", [P, TILES, P])

        rnn_ps = [psum("rnn0"), psum("rnn1")]
        a_ps, b_ps = [psum("a0"), psum("a1")], [psum("b0"), psum("b1")]
        y_ps, m_ps = psum("y_ps"), psum("m_ps")
        banks = [m_ps, rnn_ps[0], rnn_ps[1]]

        rnn_in, xw_in, moe_in, gate_in, l1_in, bias_in = (sem(n) for n in (
            "rnn_in", "xw_in", "moe_in", "gate_in", "l1_in", "bias_in"))
        ident_zero, ident_ready, ones_sq_ready, ones_ready, const_ready = (sem(n) for n in (
            "ident_zero", "ident_ready", "ones_sq_ready", "ones_ready", "const_ready"))
        z_ready, h_ready = sem("z_ready"), sem("h_ready")
        w_split, hs_split = sem("w_split"), sem("hs_split")
        b1_halved = sem("b1_halved")
        a_ready, b_ready, tanh_ready, sig_ready = (sem(n) for n in ("a_ready", "b_ready", "tanh_ready", "sig_ready"))
        p_done, hid_ready, hid_weighted, y_done = (sem(n) for n in ("p_done", "hid_ready", "hid_weighted", "y_done"))
        chunk_y, x1_ready = sem("chunk_y"), sem("x1_ready")
        exp_ready, we_ready = sem("exp_ready"), sem("we_ready")
        we_stored, we_loaded = sem("we_stored"), [sem("we_loaded0"), sem("we_loaded1")]
        filled = [sem(f"filled{n}") for n in range(3)]
        freed = [sem(f"freed{n}") for n in range(3)]
        pre_pe, pre_dve, pre_pool = sem("pre_pe"), sem("pre_dve"), sem("pre_pool")
        q_ready, gelu_ready = sem("q_ready"), sem("gelu_ready")
        q2_ready, stored = sem("q2_ready"), sem("stored")
        chain = sem("chain")

        def wait_filled(eng, kind, i):
            b, n = USES[(kind, i)]
            eng.wait_ge(filled[b], n + 1)

        def wait_free(eng, kind, i):
            b, n = USES[(kind, i)]
            if n:
                eng.wait_ge(freed[b], n)

        def wait_read(eng, kind, i):
            b, n = USES[(kind, i)]
            eng.wait_ge(freed[b], n + 1)

        def tile_cols(i):
            return slice(i * P, (i + 1) * P)

        def chunk_cols(c):
            first, n = CHUNKS[c]
            return slice(first * P, (first + n) * P)

        def expert_cols(e):
            return slice(e * P, (e + 1) * P)

        block = ctx.enter_context(nc.Block())

        @block.sync
        def _(sp):
            sp.dma_start(xT_sb[:, 0:BANK], xT[:, 0:BANK]).then_inc(xw_in, 16)
            sp.dma_start(wx_sb[:], Wx).then_inc(xw_in, 16)
            sp.dma_start(wh_sb[:], Wh).then_inc(rnn_in, 16)
            sp.dma_start(xT_sb[:, BANK:TOKENS], xT[:, BANK:TOKENS]).then_inc(rnn_in, 16)
            sp.dma_start(w1_sb[:], W1T).then_inc(moe_in, 16)
            sp.dma_start(w3_sb[:], W3T).then_inc(moe_in, 16)
            sp.dma_start(f1_sb[:], F1T).then_inc(l1_in, 16)
            sp.dma_start(f2_sb[:], F2T).then_inc(l1_in, 16)
            sp.dma_start(w2_sb[:], W2T).then_inc(gate_in, 16)
            for kind, n in SCHEDULE:
                if kind == "WB":
                    first, k = CHUNKS[n]
                    cols = chunk_cols(n)
                    wait_read(sp, "WT", first + k - 1)
                    sp.dma_start(we_dram[:, cols], weT[:, cols]).then_inc(we_stored, 16)
                    sp.wait_ge(we_stored, 16 * (n + 1))
                    if n >= 2:
                        sp.wait_ge(hid_weighted, EXPERTS * (n - 1))
                    for q in range(4):
                        sp.dma_start(we_bc[:, n % 2, 4 * q:4 * q + 4, 0:k * P],
                                     we_dram[4 * q:4 * q + 4, cols].rearrange("(o e) t -> o e t", o=1)
                                     .broadcast_to([P, 4, k * P])).then_inc(we_loaded[n % 2], 16)
                if kind == "OUT":
                    wait_read(sp, "OUT", n)
                    sp.dma_start(out[n], out_sb[:, n, :]).then_inc(stored, 16)
            sp.wait_ge(stored, 16 * TILES)

        @block.gpsimd
        def _(pool):
            pool.memset(ones_row[:], 1.0).then_inc(ones_ready, 1)
            pool.memset(ident[:], 0.0).then_inc(ident_zero, 1)
            pool.wait_ge(ident_zero, 1)
            pool.affine_select(out=ident[:], in_=ident[:], compare_op=ALU.not_equal, fill=1.0,
                               base=0, pattern=[[-1, P]], channel_multiplier=1).then_inc(ident_ready, 1)
            pool.memset(e_const[:], E_CONST).then_inc(const_ready, 1)
            pool.memset(neg_half[:], -0.5).then_inc(const_ready, 1)
            pool.wait_ge(const_ready, 2)
            pool.wait_ge(pre_dve, 2)
            pool.tensor_tensor(dT[:], d_sum[:], neg_half[:], ALU.pow).then_inc(pre_pool, 1)
            for kind, n in SCHEDULE:
                if kind == "SCORES":
                    wait_read(pool, "SCORES", n)
                    pool.tensor_tensor(exp_neg[:, n, :], e_const[:], neg_scores[:, n, :],
                                       ALU.pow).then_inc(exp_ready, 1)
                if kind == "A":
                    w = chunk_of(n)[1] * P
                    pool.wait_ge(tanh_ready, n + 1)
                    pool.tensor_scalar(gate_t[:, n % 4, 0:w], gate_t[:, n % 4, 0:w], 1.0, 0.5,
                                       ALU.add, ALU.mult).then_inc(sig_ready, 1)
                if kind == "W":
                    c, e = divmod(n, EXPERTS)
                    w = chunk_of(n)[1] * P
                    pool.wait_ge(hid_ready, n + 1)
                    pool.wait_ge(we_loaded[c % 2], 64 * (c // 2 + 1))
                    pool.tensor_tensor(hid[:, n % H_RING, 0:w], hid[:, n % H_RING, 0:w],
                                       we_bc[:, c % 2, e, 0:w], ALU.mult).then_inc(hid_weighted, 1)

        @block.scalar
        def _(act):
            act.dma_start(bh_sb[:], bh).then_inc(xw_in, 16)
            act.dma_start(h0_sb[:], h0T).then_inc(rnn_in, 16)
            act.dma_start(b1_sb[:], b1T).then_inc(bias_in, 16)
            act.dma_start(b3_sb[:], b3T).then_inc(bias_in, 16)
            act.dma_start(wg_sb[:], WgT).then_inc(gate_in, 16)
            act.dma_start(b2e_sb[:], b2e).then_inc(gate_in, 16)
            act.dma_start(cond_sb[:], condT).then_inc(l1_in, 16)
            act.dma_start(wc_sb[:], Wc).then_inc(l1_in, 16)
            act.dma_start(fb1_bc[:], fb1.broadcast_to([P, HIDDEN])).then_inc(l1_in, 16)
            act.dma_start(fb2_bc[:], fb2.broadcast_to([P, P])).then_inc(l1_in, 16)
            for kind, n in SCHEDULE:
                if kind == "RNN":
                    cols = slice(n * BATCH, (n + 1) * BATCH)
                    bank, at = divmod(n * BATCH, BANK)
                    act.wait_ge(z_ready, n + 1)
                    act.activation(hs[:, cols], rnn_ps[bank][:, at:at + BATCH], ACT.Tanh).then_inc(h_ready, 1)
                if kind == "A":
                    e = n % EXPERTS
                    w = chunk_of(n)[1] * P
                    if n == 0:
                        act.wait_ge(b1_halved, 1)
                    act.wait_ge(a_ready, n + 1)
                    act.activation(gate_t[:, n % 4, 0:w], a_ps[n % 2][:, 0:w], ACT.Tanh,
                                   bias=b1_half[:, e:e + 1], scale=0.5).then_inc(tanh_ready, 1)
                if kind == "GELU":
                    wait_read(act, "HP", n)
                    act.activation(hp[:, n % 4, :], hp[:, n % 4, :], ACT.Gelu).then_inc(gelu_ready, 1)

        @block.vector
        def _(dve):
            links = [0]

            def link(ins):
                links[0] += 1
                ins.then_inc(chain, 1)
                dve.wait_ge(chain, links[0])

            dve.memset(zeros16[:], 0.0)
            dve.memset(gmax[:], -1.0)
            dve.memset(ones_sq[:], 1.0).then_inc(ones_sq_ready, 1)
            dve.wait_ge(bias_in, 32)
            dve.tensor_scalar(b1_half[:], b1_sb[:], 0.5, None, ALU.mult).then_inc(b1_halved, 1)
            dve.wait_ge(l1_in, 96)
            link(dve.tensor_scalar(ysT[:], cond_sb[:], float(P) ** -0.5, None, ALU.mult))
            dve.tensor_tensor(ys2[:], ysT[:], ysT[:], ALU.mult)
            dve.tensor_tensor(wc2[:], wc_sb[:], wc_sb[:], ALU.mult)
            dve.tensor_reduce(f_abs[:, 0:1], f1_sb[:], AX_X, ALU.add, apply_absolute_value=True)
            link(dve.tensor_reduce(f_abs[:, 1:2], f2_sb[:], AX_X, ALU.add, apply_absolute_value=True))
            dve.wait_ge(ident_ready, 1)
            dve.tensor_copy(ident_bf[:], ident[:]).then_inc(pre_dve, 1)
            dve.wait_ge(pre_dve, 1)
            dve.wait_ge(pre_pe, 1)
            dve.tensor_scalar(d_sum[:], m_ps[:, 0:BATCH], 1e-8, None, ALU.add).then_inc(pre_dve, 1)
            link(dve.tensor_scalar(f_scale[:], m_ps[:, BATCH:BATCH + 2], 1.0 / (P * HIDDEN), 1e-5, ALU.mult, ALU.max))
            dve.tensor_scalar(f_scale_q[:], f_scale[:], 1.0 / QB, None, ALU.mult)
            link(dve.reciprocal(f_inv[:], f_scale[:]))
            for k, (src, dst) in enumerate(((f1_sb[:], f1_q[:]), (f2_sb[:], f2_q[:].rearrange("p a b -> p (a b)")))):
                link(dve.tensor_scalar(src, src, f_inv[:, k:k + 1], MAGIC, ALU.mult, ALU.add))
                link(dve.tensor_scalar(src, src, MAGIC, -1.0, ALU.subtract, ALU.max))
                link(dve.tensor_scalar(dst, src, 1.0, None, ALU.min))
            dve.wait_ge(pre_pool, 1)
            dve.tensor_copy(dT_rep[:].rearrange("p (t b) -> p t b", b=BATCH),
                            dT[:].rearrange("p (o b) -> p o b", o=1).broadcast_to([P, STEPS_PER_TILE, BATCH])).then_inc(pre_dve, 1)
            dve.wait_ge(pre_pe, 2)
            dve.tensor_copy(demod[:], m_ps[:, 0:P]).then_inc(pre_dve, 1)
            dve.wait_ge(moe_in, 32)
            for src, hi, lo in ((w1_sb, w1_hi, w1_lo), (w3_sb, w3_hi, w3_lo)):
                for q in range(4):
                    cols = slice(q * BANK, (q + 1) * BANK)
                    link(dve.tensor_copy(hi[:, cols], src[:, cols]))
                    dve.tensor_tensor(lo[:, cols], src[:, cols], hi[:, cols].bitcast(F32), ALU.subtract).then_inc(w_split, 1)

            def select_top(values, n, k, sel):
                link(dve.max(top8[:], values))
                least = top8[:, k - 1:k]
                v = values[:, 0:n]
                dve.tensor_scalar(above[:, 0:n], v, least, None, ALU.is_gt)
                link(dve.tensor_scalar(equal[:, 0:n], v, least, None, ALU.is_equal))
                dve.tensor_reduce(n_above[:], above[:, 0:n], AX_X, ALU.add)
                link(dve.tensor_tensor_scan(before[:, 0:n], equal[:, 0:n], zeros16[:, 0:n], 0.0, ALU.add, ALU.add))
                link(dve.tensor_scalar(fits[:, 0:n], before[:, 0:n], n_above[:], float(k), ALU.add, ALU.is_le))
                link(dve.tensor_tensor(fits[:, 0:n], fits[:, 0:n], equal[:, 0:n], ALU.mult))
                link(dve.tensor_tensor(sel, fits[:, 0:n], above[:, 0:n], ALU.add))

            def by_group(ap):
                return ap.rearrange("p (g e) -> p g e", g=GROUPS)

            def quantise_scale(slot):
                a = slice(slot, slot + 1)
                which = slice(slot % 2, slot % 2 + 1)
                link(dve.tensor_scalar(xs[:, a], amax[:, a], 1e-5, None, ALU.max))
                dve.tensor_scalar(deq[:, a], xs[:, a], f_scale_q[:, which], None, ALU.mult)
                link(dve.reciprocal(xinv[:, a], xs[:, a]))
                link(dve.tensor_scalar(x127[:, a], xinv[:, a], QB, None, ALU.mult))

            for kind, n in SCHEDULE:
                if kind == "SCORES":
                    wait_filled(dve, kind, n)
                    dve.tensor_scalar(neg_scores[:, n, :], m_ps[:, 0:EXPERTS], -1.0, None, ALU.mult).then_inc(freed[M], 1)
                if kind == "SPLIT":
                    cols = chunk_cols(n)
                    dve.wait_ge(h_ready, (CHUNKS[n][0] + CHUNKS[n][1]) * STEPS_PER_TILE)
                    link(dve.tensor_copy(hs_hi[:, cols], hs[:, cols]))
                    dve.tensor_tensor(hs_lo[:, cols], hs[:, cols], hs_hi[:, cols].bitcast(F32), ALU.subtract).then_inc(hs_split, 1)
                if kind == "GATE":
                    dve.wait_ge(exp_ready, n + 1)
                    link(dve.tensor_scalar(s_gate[:], exp_neg[:, n, :], 1.0, None, ALU.add))
                    link(dve.reciprocal(s_gate[:], s_gate[:]))
                    link(dve.tensor_reduce(gmax[:, 0:GROUPS], by_group(s_gate[:]), AX_X, ALU.max))
                    select_top(gmax[:], GROUPS, TOP_GROUPS, g_sel[:])
                    g = g_sel[:].rearrange("p (g o) -> p g o", o=1).broadcast_to([P, GROUPS, EXPERTS // GROUPS])
                    link(dve.tensor_tensor(by_group(masked[:]), by_group(s_gate[:]), g, ALU.mult))
                    link(dve.scalar_tensor_tensor(out=by_group(masked[:]), in0=g, scalar=-1.0, in1=by_group(masked[:]),
                                                  op0=ALU.add, op1=ALU.add))
                    select_top(masked[:], EXPERTS, TOP_EXPERTS, e_sel[:])
                    link(dve.tensor_tensor(w_raw[:], e_sel[:], s_gate[:], ALU.mult))
                    link(dve.tensor_reduce(w_sum[:], w_raw[:], AX_X, ALU.add))
                    link(dve.reciprocal(w_inv[:], w_sum[:]))
                    dve.tensor_scalar(we[:, n, :], w_raw[:], w_inv[:], ROUTE_SCALE, ALU.mult, ALU.mult).then_inc(we_ready, 1)
                if kind == "WT":
                    wait_filled(dve, kind, n)
                    dve.tensor_copy(weT[:, tile_cols(n)], m_ps[0:EXPERTS, 0:P]).then_inc(freed[M], 1)
                if kind == "B":
                    e = n % EXPERTS
                    w = chunk_of(n)[1] * P
                    h = hid[:, n % H_RING, 0:w]
                    if n >= H_RING:
                        dve.wait_ge(y_done, n - H_RING + 1)
                    dve.wait_ge(sig_ready, n + 1)
                    dve.scalar_tensor_tensor(out=h, in0=a_ps[n % 2][:, 0:w], scalar=b1_sb[:, e:e + 1],
                                             in1=gate_t[:, n % 4, 0:w], op0=ALU.add, op1=ALU.mult).then_inc(p_done, 1)
                    dve.wait_ge(p_done, n + 1)
                    dve.wait_ge(b_ready, n + 1)
                    dve.scalar_tensor_tensor(out=h, in0=b_ps[n % 2][:, 0:w], scalar=b3_sb[:, e:e + 1],
                                             in1=h, op0=ALU.add, op1=ALU.mult).then_inc(hid_ready, 1)
                if kind == "FIN":
                    cols = chunk_cols(n)
                    w = CHUNKS[n][1] * P
                    if n == 0:
                        dve.wait_ge(rnn_in, 48)
                        dve.wait_ge(xw_in, 48)
                    dve.wait_ge(chunk_y, n + 1)
                    link(dve.tensor_tensor(x1T[:, cols], y_ps[:, 0:w], xT_sb[:, cols], ALU.add))
                    dve.tensor_tensor(zT[:, cols].rearrange("p (t b) -> p t b", b=BATCH),
                                      x1T[:, cols].rearrange("p (t b) -> p t b", b=BATCH),
                                      ysT[:].rearrange("p (o b) -> p o b", o=1).broadcast_to([P, w // BATCH, BATCH]),
                                      ALU.mult).then_inc(x1_ready, 1)
                if kind == "X":
                    bank = banks[bank_of(kind, n)]
                    if n == 0:
                        dve.wait_ge(l1_in, 96)
                    wait_filled(dve, kind, n)
                    dve.tensor_tensor(x1b[:, n, :], bank[:, 0:P], fb2_bc[:], ALU.add)
                    dve.tensor_tensor(o_sb[:], bank[:, P:2 * P], demod[:], ALU.mult).then_inc(freed[bank_of(kind, n)], 1)
                    wait_read(dve, kind, n)
                    link(dve.tensor_reduce(amax[:, 2 * n:2 * n + 1], o_sb[:], AX_X, ALU.max, apply_absolute_value=True))
                    quantise_scale(2 * n)
                    link(dve.tensor_scalar(q_f[:], o_sb[:], x127[:, 2 * n:2 * n + 1], MAGIC, ALU.mult, ALU.add))
                    dve.tensor_scalar(q_bf[:, n % 2, :], q_f[:], MAGIC, None, ALU.subtract).then_inc(q_ready, 1)
                if kind == "Q":
                    wait_filled(dve, kind, n)
                    dve.tensor_scalar(qT[:, n % 2, :], m_ps[:, 0:P // 2].bitcast(BF16), -QB - 1.0, QB,
                                      ALU.max, ALU.min).then_inc(freed[M], 1)
                if kind == "HP":
                    wait_filled(dve, kind, n)
                    b = bank_of(kind, n)
                    dve.scalar_tensor_tensor(out=hp[:, n % 4, :], in0=banks[b][:], scalar=deq[:, 2 * n:2 * n + 1],
                                             in1=fb1_bc[:], op0=ALU.mult, op1=ALU.add).then_inc(freed[b], 1)
                if kind == "Q2":
                    s = 2 * n + 1
                    dve.wait_ge(gelu_ready, n + 1)
                    link(dve.tensor_reduce(amax[:, s:s + 1], hp[:, n % 4, :], AX_X, ALU.max, apply_absolute_value=True))
                    quantise_scale(s)
                    link(dve.tensor_scalar(q2_f[:], hp[:, n % 4, :], x127[:, s:s + 1], MAGIC, ALU.mult, ALU.add))
                    dve.tensor_scalar(q2_bf[:, n % 2, :], q2_f[:], MAGIC, None, ALU.subtract).then_inc(q2_ready, 1)
                if kind == "T2":
                    b = bank_of(kind, n)
                    wait_filled(dve, kind, n)
                    dve.tensor_scalar(q2T[:, n % 2, :], banks[b][:, 0:HIDDEN // 2].bitcast(BF16), -QB - 1.0, QB,
                                      ALU.max, ALU.min).then_inc(freed[b], 1)
                if kind == "OUT":
                    b = bank_of(kind, n)
                    wait_filled(dve, kind, n)
                    dve.scalar_tensor_tensor(out=out_sb[:, n, :], in0=banks[b][:, 0:P], scalar=deq[:, 2 * n + 1:2 * n + 2],
                                             in1=x1b[:, n, :], op0=ALU.mult, op1=ALU.add).then_inc(freed[b], 1)

        @block.tensor
        def _(pe):
            pe.wait_ge(xw_in, 48)
            pe.matmul(rnn_ps[0][:], wx_sb[:], xT_sb[:, 0:BANK], start=True, stop=False, skip_group_check=True)
            pe.wait_ge(ones_ready, 1)
            pe.matmul(rnn_ps[0][:], bh_sb[:], ones_row[:], start=False, stop=False, skip_group_check=True)

            def second_bank():
                pe.matmul(rnn_ps[1][:], wx_sb[:], xT_sb[:, BANK:TOKENS], start=True, stop=False, skip_group_check=True)
                pe.matmul(rnn_ps[1][:], bh_sb[:], ones_row[:], start=False, stop=False, skip_group_check=True)

            def demodulation():
                pe.wait_ge(ones_sq_ready, 1)
                pe.wait_ge(pre_dve, 1)
                pe.matmul(m_ps[:, 0:BATCH], wc2[:], ys2[:], start=True, stop=True, skip_group_check=True)
                pe.matmul(m_ps[:, BATCH:BATCH + 2], ones_sq[:], f_abs[:], start=True, stop=True,
                          skip_group_check=True).then_inc(pre_pe, 1)

            def demod_rows():
                pe.wait_ge(pre_dve, 3)
                pe.transpose(m_ps[:, 0:P], dT_rep[:], ident[:]).then_inc(pre_pe, 1)

            def products(ps, w32, hi, lo, j):
                c, e = divmod(j, EXPERTS)
                cols, ex = chunk_cols(c), expert_cols(e)
                w = CHUNKS[c][1] * P
                if CHUNKS[c][1] == 1:
                    return pe.matmul(ps[:, 0:w], w32[:, ex], hs[:, cols], start=True, stop=True)
                pe.matmul(ps[:, 0:w], lo[:, ex], hs_hi[:, cols], start=True, stop=False)
                pe.matmul(ps[:, 0:w], hi[:, ex], hs_lo[:, cols], start=False, stop=False)
                return pe.matmul(ps[:, 0:w], hi[:, ex], hs_hi[:, cols], start=False, stop=True)

            for kind, n in SCHEDULE:
                if kind == "RNN":
                    bank, at = divmod(n * BATCH, BANK)
                    if n == 0:
                        pe.wait_ge(rnn_in, 48)
                    else:
                        pe.wait_ge(h_ready, n)
                    prev = h0_sb[:] if n == 0 else hs[:, (n - 1) * BATCH:n * BATCH]
                    pe.matmul(rnn_ps[bank][:, at:at + BATCH], wh_sb[:], prev, start=False, stop=True,
                              skip_group_check=True).then_inc(z_ready, 1)
                    if n == 0:
                        second_bank()
                    if n == 8:
                        demodulation()
                    if n == 14:
                        demod_rows()
                if kind == "SCORES":
                    if n == 0:
                        pe.wait_ge(gate_in, 48)
                        pe.wait_ge(pre_dve, 4)
                    if n == TILES - 1:
                        pe.wait_ge(h_ready, STEPS)
                    wait_free(pe, kind, n)
                    pe.matmul(m_ps[:, 0:EXPERTS], hs[:, tile_cols(n)], wg_sb[:], start=True, stop=True).then_inc(filled[M], 1)
                if kind == "WT":
                    pe.wait_ge(we_ready, n + 1)
                    wait_free(pe, kind, n)
                    pe.transpose(m_ps[0:EXPERTS, 0:P], we[:, n, :], ident[:]).then_inc(filled[M], 1)
                if kind == "A":
                    c = n // EXPERTS
                    if n == 0:
                        pe.wait_ge(moe_in, 32)
                    if CHUNKS[c][1] > 1:
                        first_big = min(k for k, ch in enumerate(CHUNKS) if ch[1] > 1)
                        pe.wait_ge(w_split, 8)
                        pe.wait_ge(hs_split, c - first_big + 1)
                    if n >= 2:
                        pe.wait_ge(p_done, n - 1)
                    products(a_ps[n % 2], w1_sb, w1_hi, w1_lo, n).then_inc(a_ready, 1)
                if kind == "B":
                    if n >= 2:
                        pe.wait_ge(hid_ready, n - 1)
                    products(b_ps[n % 2], w3_sb, w3_hi, w3_lo, n).then_inc(b_ready, 1)
                if kind == "Y":
                    c, e = divmod(n, EXPERTS)
                    w = chunk_of(n)[1] * P
                    if e == 0 and c:
                        pe.wait_ge(x1_ready, c)
                    pe.wait_ge(hid_weighted, n + 1)
                    pe.matmul(y_ps[:, 0:w], w2_sb[:, expert_cols(e)], hid[:, n % H_RING, 0:w],
                              start=(e == 0), stop=False).then_inc(y_done, 1)
                if kind == "FIN":
                    wait_read(pe, "WT", CHUNKS[n][0] + CHUNKS[n][1] - 1)
                    pe.matmul(y_ps[:, 0:CHUNKS[n][1] * P], b2e_sb[:], weT[:, chunk_cols(n)],
                              start=False, stop=True).then_inc(chunk_y, 1)
                if kind == "X":
                    bank = banks[bank_of(kind, n)]
                    c = next(k for k, (first, m) in enumerate(CHUNKS) if first <= n < first + m)
                    pe.wait_ge(x1_ready, c + 1)
                    wait_free(pe, kind, n)
                    pe.transpose(bank[:, 0:P], x1T[:, tile_cols(n)], ident[:])
                    pe.matmul(bank[:, P:2 * P], zT[:, tile_cols(n)], wc_sb[:], start=True, stop=True,
                              skip_group_check=True).then_inc(filled[bank_of(kind, n)], 1)
                if kind == "Q":
                    pe.wait_ge(q_ready, n + 1)
                    wait_free(pe, kind, n)
                    pe.transpose(m_ps[:, 0:P // 2].bitcast(BF16), q_bf[:, n % 2, :], ident_bf[:]).then_inc(filled[M], 1)
                if kind == "HP":
                    b = bank_of(kind, n)
                    wait_read(pe, "Q", n)
                    wait_free(pe, kind, n)
                    pe.matmul(banks[b][:], qT[:, n % 2, :], f1_q[:], start=True, stop=True).then_inc(filled[b], 1)
                if kind == "T2":
                    b = bank_of(kind, n)
                    pe.wait_ge(q2_ready, n + 1)
                    wait_free(pe, kind, n)
                    for k in range(HB):
                        last = pe.transpose(banks[b][:, k * P // 2:(k + 1) * P // 2].bitcast(BF16),
                                            q2_bf[:, n % 2, k * P:(k + 1) * P], ident_bf[:])
                    last.then_inc(filled[b], 1)
                if kind == "OUT":
                    b = bank_of(kind, n)
                    wait_read(pe, "T2", n)
                    wait_free(pe, kind, n)
                    for k in range(HB):
                        last = pe.matmul(banks[b][:, 0:P], q2T[:, n % 2, k * P:(k + 1) * P], f2_q[:, k, :],
                                         start=(k == 0), stop=(k == HB - 1))
                    last.then_inc(filled[b], 1)


def kernel(x, cond_1024, L0_cond_Wx, L0_cond_Wh, L0_cond_b, L0_ffn_Wg, L0_ffn_W1, L0_ffn_b1,
           L0_ffn_W2, L0_ffn_b2, L0_ffn_W3, L0_ffn_b3, L1_cond_weight, L1_ffn_W1, L1_ffn_b1,
           L1_ffn_W2, L1_ffn_b2):
    import numpy as np
    import concourse.bacc as bacc
    from concourse.bass_utils import run_bass_kernel_spmd

    def lay(a, *shape):
        return np.ascontiguousarray(a).reshape(shape)

    x = np.asarray(x)
    by_step = x.transpose(1, 0, 2).reshape(TOKENS, P)
    cond = np.asarray(cond_1024)
    experts = lambda w: lay(np.asarray(w).transpose(2, 0, 1), P, EXPERTS * P)
    arrays = {
        "xT": lay(by_step.T, P, TOKENS),
        "h0T": lay(cond.T, P, BATCH),
        "Wx": lay(L0_cond_Wx, P, P),
        "Wh": lay(L0_cond_Wh, P, P),
        "bh": lay(L0_cond_b, 1, P),
        "WgT": lay(np.asarray(L0_ffn_Wg).T, P, EXPERTS),
        "W1T": experts(L0_ffn_W1),
        "W3T": experts(L0_ffn_W3),
        "W2T": experts(L0_ffn_W2),
        "b1T": lay(np.asarray(L0_ffn_b1).T, P, EXPERTS),
        "b3T": lay(np.asarray(L0_ffn_b3).T, P, EXPERTS),
        "b2e": lay(L0_ffn_b2, EXPERTS, P),
        "condT": lay(cond.T, P, BATCH),
        "Wc": lay(L1_cond_weight, P, P),
        "F1T": lay(np.asarray(L1_ffn_W1).T, P, HIDDEN),
        "F2T": lay(np.asarray(L1_ffn_W2).T.reshape(HB, P, P).transpose(1, 0, 2), P, HIDDEN),
        "fb1": lay(L1_ffn_b1, 1, HIDDEN),
        "fb2": lay(L1_ffn_b2, 1, P),
    }
    nc = bacc.Bacc("TRN2", target_bir_lowering=False, num_devices=1)
    aps = {name: nc.dram_tensor(name, a.shape, F32, kind="ExternalInput").ap() for name, a in arrays.items()}
    we_dram = nc.dram_tensor("we_dram", (EXPERTS, TOKENS), F32, kind="Internal").ap()
    out = nc.dram_tensor("out", (TILES, P, P), F32, kind="ExternalOutput").ap()
    adaln_ffn(nc, None, we_dram=we_dram, out=out, **aps)
    r = run_bass_kernel_spmd(nc, [arrays], core_ids=[0])
    y = r.results[0]["out"]
    return np.ascontiguousarray(y.reshape(STEPS, BATCH, P).transpose(1, 0, 2))
```

```python
from contextlib import ExitStack

import concourse.bass as bass
from concourse import mybir

ALU = mybir.AluOpType
ACT = mybir.ActivationFunctionType
AX_X = mybir.AxisListType.X
F32 = mybir.dt.float32
F32R = mybir.dt.float32r
BF16 = mybir.dt.bfloat16

P = 128
BATCH = 8
STEPS = 128
TOKENS = BATCH * STEPS
TILES = TOKENS // P
STEPS_PER_TILE = P // BATCH
BANK = 512
EXPERTS = 16
GROUPS = 4
TOP_GROUPS = 2
TOP_EXPERTS = 4
ROUTE_SCALE = 2.5
QB = 127.0
HIDDEN = 512
HB = HIDDEN // P
MAGIC = 1.5 * 2.0 ** 23
E_CONST = 2.718281828459045

CHUNKS = [(0, 1), (1, 1), (2, 2), (4, 2), (6, 2)]
LAST_CHUNK = len(CHUNKS) - 1
JOBS = len(CHUNKS) * EXPERTS
H_RING = 24
GATE_STAGES = 21
EXP_PARTS = 4
SETUP_STAGES = 10

SETUP_AT = 20.0
JOB_TIME = {1: 1.5, 2: 2.5}
TAIL_JOB_TIME = 1.65
EXP_AT, EXP_TIME = 1.4, 1.3
GATE_AT, GATE_TIME = 2.0, 0.4
WEIGHTS_AT = 7.0
L1_TIMES = {"X": 0.0, "X_READ": 1.0, "AMAX1": 1.6, "SCALE1": 2.2, "RECIP1": 2.7, "ROUND1": 3.3,
            "INT1": 3.9, "Q": 5.5, "Q_READ": 6.5, "HP": 8.0, "HP_READ": 9.0, "GELU": 10.0,
            "AMAX2": 11.5, "SCALE2": 12.3, "RECIP2": 12.8, "ROUND2": 13.4, "INT2": 14.0,
            "T2": 16.0, "T2_READ": 16.5, "OUT": 18.5, "OUT_READ": 19.5}


def chunk_of(j):
    return CHUNKS[j // EXPERTS]


def chunk_with(i):
    return next(c for c, (first, n) in enumerate(CHUNKS) if first <= i < first + n)


def build_schedule():
    timed = []

    def at(time, kind, n):
        timed.append((time, len(timed), kind, n))

    for t in range(STEPS):
        at(t, "RNN", t)
    for d in range(SETUP_STAGES):
        at(SETUP_AT + d, "SETUP", d)
    exp_free = 0.0
    product_time = down_time = 0.0
    for c, (first, n) in enumerate(CHUNKS):
        for i in range(first, first + n):
            done = (i + 1) * STEPS_PER_TILE
            at(done + 0.1, "SCORES", i)
            at(done + 1.2, "SCORES_READ", i)
            exp_free = max(exp_free, done + EXP_AT)
            for q in range(EXP_PARTS):
                at(exp_free, "EXP", i * EXP_PARTS + q)
                exp_free += EXP_TIME
        done = (first + n) * STEPS_PER_TILE
        if n > 1:
            at(done + 0.2, "SPLIT", c)
        gate = exp_free + GATE_AT
        for d in range(GATE_STAGES):
            at(gate + d * GATE_TIME, "GATE", c * GATE_STAGES + d)
        gate += GATE_STAGES * GATE_TIME + 1.0
        for i in range(first, first + n):
            at(gate, "WT", i)
            at(gate + 1.0, "WT_READ", i)
            gate += 1.5
        at(gate, "WB", c)
        weighted = gate + WEIGHTS_AT
        product_time = max(product_time, done + 0.5)
        for e in range(EXPERTS):
            j = c * EXPERTS + e
            long = JOB_TIME[n] if product_time < STEPS else TAIL_JOB_TIME
            at(product_time, "A", j)
            at(product_time + long / 3, "B", j)
            at(product_time + 1.7, "GATED", j)
            at(product_time + 2.3, "HIDDEN", j)
            down_time = max(down_time, product_time + 5, weighted)
            at(down_time, "W", j)
            at(down_time + 3.0, "Y", j)
            product_time += long
            down_time += long
        fin = down_time + 3.0
        at(fin, "FIN", c)
        at(fin + 0.8, "FIN_READ", c)
        start = max(fin + 2.5, STEPS / 2 + 1)
        for m in range(n):
            for kind, offset in L1_TIMES.items():
                at(start + 3 * m + offset, kind, first + m)
    return [(kind, n) for _, _, kind, n in sorted(timed)]


SCHEDULE = build_schedule()

M, R0, R1 = range(3)


def bank_of(kind, i):
    if kind in ("SCORES", "WT", "Q"):
        return M
    if kind in ("X", "HP"):
        return R1 if i == TILES - 1 else R0
    return R1 if i == TILES - 1 else M


def bank_uses():
    count, place = [0, 0, 0], {}
    for kind, i in SCHEDULE:
        if kind in ("SCORES", "WT", "X", "Q", "HP", "T2", "OUT"):
            b = bank_of(kind, i)
            place[(kind, i)] = (b, count[b])
            count[b] += 1
    return place


USES = bank_uses()


def adaln_ffn(nc, x_nat, xT, h0T, Wx, Wh, bh, WgT, W1T, W3T, W2T, b1T, b3T, b2e,
              condT, Wc, F1T, F2T, fb1, fb2, we_dram, out):
    with ExitStack() as ctx:
        def sb(name, shape, dt=F32):
            return ctx.enter_context(nc.sbuf_tensor(name, shape, dt))

        def psum(name):
            return ctx.enter_context(nc.psum_tensor(name, [P, BANK], F32))

        def sem(name):
            return ctx.enter_context(nc.semaphore(name))

        xT_sb = sb("xT_sb", [P, TOKENS])
        xn_sb = None
        h0_sb = sb("h0_sb", [P, BATCH])
        wx_sb, wh_sb = sb("wx_sb", [P, P]), sb("wh_sb", [P, P])
        bh_sb = sb("bh_sb", [1, P])
        ones_row = sb("ones_row", [1, BANK])
        hs = sb("hs", [P, TOKENS])
        hs_hi, hs_lo = sb("hs_hi", [P, TOKENS], F32R), sb("hs_lo", [P, TOKENS], F32R)
        w1_sb, w3_sb = sb("w1_sb", [P, EXPERTS * P]), sb("w3_sb", [P, EXPERTS * P])
        w2_sb = sb("w2_sb", [P, EXPERTS * P])
        w1_hi, w1_lo = sb("w1_hi", [P, EXPERTS * P], F32R), sb("w1_lo", [P, EXPERTS * P], F32R)
        w3_hi, w3_lo = sb("w3_hi", [P, EXPERTS * P], F32R), sb("w3_lo", [P, EXPERTS * P], F32R)
        b1_sb, b1_half, b3_sb = sb("b1_sb", [P, EXPERTS]), sb("b1_half", [P, EXPERTS]), sb("b3_sb", [P, EXPERTS])
        b2e_sb = sb("b2e_sb", [EXPERTS, P])
        wg_sb = sb("wg_sb", [P, EXPERTS])
        gate_t = sb("gate_t", [P, 4, 256])
        gate_a = sb("gate_a", [P, 4, 256])
        hid = sb("hid", [P, H_RING, 256])
        we_bc = sb("we_bc", [P, 2, EXPERTS, 256])
        weT = sb("weT", [EXPERTS, TOKENS])
        e_const = sb("e_const", [P, EXPERTS])
        neg_scores, exp_neg = sb("neg_scores", [P, TILES, EXPERTS]), sb("exp_neg", [P, TILES, EXPERTS])
        s_gate, masked, w_raw = (sb(n, [P, 2, EXPERTS]) for n in ("s_gate", "masked", "w_raw"))
        gmax, top8 = sb("gmax", [P, 2, 8]), sb("top8", [P, 2, 8])
        above, equal, before, fits = (sb(n, [P, 2, EXPERTS]) for n in ("above", "equal", "before", "fits"))
        g_sel, e_sel = sb("g_sel", [P, 2, GROUPS]), sb("e_sel", [P, 2, EXPERTS])
        n_above, w_sum, w_inv = (sb(n, [P, 2]) for n in ("n_above", "w_sum", "w_inv"))
        zeros16 = sb("zeros16", [P, EXPERTS])
        we = sb("we", [P, TILES, EXPERTS])
        x1T, zT = sb("x1T", [P, TOKENS]), sb("zT", [P, TOKENS])
        cond_sb, ysT, ys2 = sb("cond_sb", [P, BATCH]), sb("ysT", [P, BATCH]), sb("ys2", [P, BATCH])
        wc_sb, wc2 = sb("wc_sb", [P, P]), sb("wc2", [P, P])
        neg_half, d_sum, dT = sb("neg_half", [P, BATCH]), sb("d_sum", [P, BATCH]), sb("dT", [P, BATCH])
        dT_rep = sb("dT_rep", [P, P])
        demod = sb("demod", [P, P])
        f1_sb, f2_sb = sb("f1_sb", [P, HIDDEN]), sb("f2_sb", [P, HIDDEN])
        f1_q, f2_q = sb("f1_q", [P, HIDDEN], BF16), sb("f2_q", [P, HB, P], BF16)
        f_abs, f_scale, f_inv = (sb(n, [P, 2]) for n in ("f_abs", "f_scale", "f_inv"))
        fb1_bc, fb2_bc = sb("fb1_bc", [P, HIDDEN]), sb("fb2_bc", [P, P])
        ident, ident_bf, ones_sq = sb("ident", [P, P]), sb("ident_bf", [P, P], BF16), sb("ones_sq", [P, P])
        x1b = sb("x1b", [P, TILES, P])
        o_sb, q_f = sb("o_sb", [P, 2, P]), sb("q_f", [P, 2, P])
        q_bf, qT = sb("q_bf", [P, 2, P], BF16), sb("qT", [P, 2, P], BF16)
        amax, step, inv_step, deq = (sb(n, [P, 2 * TILES]) for n in ("amax", "step", "inv_step", "deq"))
        hp = sb("hp", [P, 4, HIDDEN])
        q2_f, q2_bf, q2T = sb("q2_f", [P, 2, HIDDEN]), sb("q2_bf", [P, 2, HIDDEN], BF16), sb("q2T", [P, 2, HIDDEN], BF16)
        out_sb = sb("out_sb", [P, TILES, P])

        rnn_ps = [psum("rnn0"), psum("rnn1")]
        a_ps, b_ps = [psum("a0"), psum("a1")], [psum("b0"), psum("b1")]
        y_ps, m_ps = psum("y_ps"), psum("m_ps")
        banks = [m_ps, rnn_ps[0], rnn_ps[1]]

        rnn_in, xw_in, x_in, moe_in, gate_in, l1_in, bias_in = (sem(n) for n in (
            "rnn_in", "xw_in", "x_in", "moe_in", "gate_in", "l1_in", "bias_in"))
        ident_zero, ident_ready, ones_sq_ready, ones_ready, const_ready = (sem(n) for n in (
            "ident_zero", "ident_ready", "ones_sq_ready", "ones_ready", "const_ready"))
        z_ready, h_ready = sem("z_ready"), sem("h_ready")
        w1_split, w3_hi_ready, w3_split, hs_split = (sem(n) for n in ("w1_split", "w3_hi_ready", "w3_split", "hs_split"))
        b1_halved, b2_doubled = sem("b1_halved"), sem("b2_doubled")
        a_ready, b_ready, gate_ready, gated = (sem(n) for n in ("a_ready", "b_ready", "gate_ready", "gated"))
        hid_ready, hid_weighted, y_done = (sem(n) for n in ("hid_ready", "hid_weighted", "y_done"))
        chunk_y, x1_ready = sem("chunk_y"), sem("x1_ready")
        exp_ready = sem("exp_ready")
        gate_step = sem("gate_step")
        we_stored, we_loaded = sem("we_stored"), [sem("we_loaded0"), sem("we_loaded1")]
        filled = [sem(f"filled{n}") for n in range(3)]
        freed = [sem(f"freed{n}") for n in range(3)]
        setup_pe, setup_dve, setup_pool = sem("setup_pe"), sem("setup_dve"), sem("setup_pool")
        q_ready, gelu_ready = sem("q_ready"), sem("gelu_ready")
        q2_ready, stored = sem("q2_ready"), sem("stored")
        chain = sem("chain")

        def wait_filled(eng, kind, i):
            b, n = USES[(kind, i)]
            eng.wait_ge(filled[b], n + 1)

        def wait_free(eng, kind, i):
            b, n = USES[(kind, i)]
            if n:
                eng.wait_ge(freed[b], n)

        def wait_read(eng, kind, i):
            b, n = USES[(kind, i)]
            eng.wait_ge(freed[b], n + 1)

        def rnn_bank(token, n):
            if token < P:
                return m_ps[:, token:token + n]
            bank, at = divmod(token, BANK)
            return rnn_ps[bank][:, at:at + n]

        def tile_cols(i):
            return slice(i * P, (i + 1) * P)

        def chunk_cols(c):
            first, n = CHUNKS[c]
            return slice(first * P, (first + n) * P)

        def expert_cols(e):
            return slice(e * P, (e + 1) * P)

        block = ctx.enter_context(nc.Block())

        @block.sync
        def _(sp):
            sp.dma_start(xT_sb[:, 0:P], xT[:, 0:P]).then_inc(xw_in, 16)
            sp.dma_start(wx_sb[:], Wx).then_inc(xw_in, 16)
            sp.dma_start(wh_sb[:], Wh).then_inc(rnn_in, 16)
            sp.dma_start(xT_sb[:, P:TOKENS], xT[:, P:TOKENS]).then_inc(x_in, 16)
            sp.dma_start(w1_sb[:], W1T).then_inc(moe_in, 16)
            sp.dma_start(w3_sb[:], W3T).then_inc(moe_in, 16)
            sp.dma_start(f1_sb[:], F1T).then_inc(l1_in, 16)
            sp.dma_start(f2_sb[:], F2T).then_inc(l1_in, 16)
            sp.dma_start(w2_sb[:], W2T).then_inc(gate_in, 16)
            for kind, n in SCHEDULE:
                if kind == "WB":
                    first, k = CHUNKS[n]
                    cols = chunk_cols(n)
                    wait_read(sp, "WT", first + k - 1)
                    sp.dma_start(we_dram[:, cols], weT[:, cols]).then_inc(we_stored, 16)
                    sp.wait_ge(we_stored, 16 * (n + 1))
                    if n >= 2:
                        sp.wait_ge(hid_weighted, EXPERTS * (n - 1))
                    for q in range(4):
                        sp.dma_start(we_bc[:, n % 2, 4 * q:4 * q + 4, 0:k * P],
                                     we_dram[4 * q:4 * q + 4, cols].rearrange("(o e) t -> o e t", o=1)
                                     .broadcast_to([P, 4, k * P])).then_inc(we_loaded[n % 2], 16)
                if kind == "OUT":
                    wait_read(sp, "OUT", n)
                    sp.dma_start(out[n], out_sb[:, n, :]).then_inc(stored, 16)
            sp.wait_ge(stored, 16 * TILES)

        @block.gpsimd
        def _(pool):
            pool.memset(ones_row[:], 1.0).then_inc(ones_ready, 1)
            pool.memset(ident[:], 0.0).then_inc(ident_zero, 1)
            pool.wait_ge(ident_zero, 1)
            pool.affine_select(out=ident[:], in_=ident[:], compare_op=ALU.not_equal, fill=1.0,
                               base=0, pattern=[[-1, P]], channel_multiplier=1).then_inc(ident_ready, 1)
            pool.memset(e_const[:], E_CONST).then_inc(const_ready, 1)
            pool.memset(neg_half[:], -0.5).then_inc(const_ready, 1)
            pool.wait_ge(const_ready, 2)
            for q in range(EXPERTS * P // BANK):
                cols = slice(q * BANK, (q + 1) * BANK)
                pool.wait_ge(w3_hi_ready, q + 1)
                pool.tensor_tensor(w3_lo[:, cols], w3_sb[:, cols], w3_hi[:, cols].bitcast(F32), ALU.subtract).then_inc(w3_split, 1)
            for kind, n in SCHEDULE:
                if (kind, n) == ("SETUP", 3):
                    pool.wait_ge(setup_dve, 4)
                    pool.tensor_tensor(dT[:], d_sum[:], neg_half[:], ALU.pow).then_inc(setup_pool, 1)
                if kind == "EXP":
                    i, q = divmod(n, EXP_PARTS)
                    part = slice(q * EXPERTS // EXP_PARTS, (q + 1) * EXPERTS // EXP_PARTS)
                    wait_read(pool, "SCORES", i)
                    pool.tensor_tensor(exp_neg[:, i, part], e_const[:, part], neg_scores[:, i, part],
                                       ALU.pow).then_inc(exp_ready, 1)
                if kind == "W":
                    c, e = divmod(n, EXPERTS)
                    w = chunk_of(n)[1] * P
                    pool.wait_ge(hid_ready, n + 1)
                    pool.wait_ge(we_loaded[c % 2], 64 * (c // 2 + 1))
                    pool.tensor_tensor(hid[:, n % H_RING, 0:w], hid[:, n % H_RING, 0:w],
                                       we_bc[:, c % 2, e, 0:w], ALU.mult).then_inc(hid_weighted, 1)

        @block.scalar
        def _(act):
            act.dma_start(bh_sb[:], bh).then_inc(xw_in, 16)
            act.dma_start(h0_sb[:], h0T).then_inc(rnn_in, 16)
            act.dma_start(b1_sb[:], b1T).then_inc(bias_in, 16)
            act.dma_start(b3_sb[:], b3T).then_inc(bias_in, 16)
            act.dma_start(wg_sb[:], WgT).then_inc(gate_in, 16)
            act.dma_start(b2e_sb[:], b2e).then_inc(gate_in, 16)
            act.dma_start(cond_sb[:], condT).then_inc(l1_in, 16)
            act.dma_start(wc_sb[:], Wc).then_inc(l1_in, 16)
            act.dma_start(fb1_bc[:], fb1.broadcast_to([P, HIDDEN])).then_inc(l1_in, 16)
            act.dma_start(fb2_bc[:], fb2.broadcast_to([P, P])).then_inc(l1_in, 16)
            for kind, n in SCHEDULE:
                if kind == "RNN":
                    cols = slice(n * BATCH, (n + 1) * BATCH)
                    act.wait_ge(z_ready, n + 1)
                    act.activation(hs[:, cols], rnn_bank(n * BATCH, BATCH), ACT.Tanh).then_inc(h_ready, 1)
                if kind == "A":
                    e = n % EXPERTS
                    w = chunk_of(n)[1] * P
                    if n == 0:
                        act.wait_ge(b1_halved, 1)
                    if n >= 4:
                        act.wait_ge(gated, n - 3)
                    act.wait_ge(a_ready, n + 1)
                    act.activation(gate_t[:, n % 4, 0:w], a_ps[n % 2][:, 0:w], ACT.Tanh,
                                   bias=b1_half[:, e:e + 1], scale=0.5)
                    act.activation(gate_a[:, n % 4, 0:w], a_ps[n % 2][:, 0:w], ACT.Identity,
                                   bias=b1_sb[:, e:e + 1]).then_inc(gate_ready, 1)
                if kind == "T2_READ":
                    b = bank_of("T2", n)
                    wait_filled(act, "T2", n)
                    act.activation(q2T[:, n % 2, :], banks[b][:, 0:HIDDEN // 2].bitcast(BF16), ACT.Copy).then_inc(freed[b], 1)
                if kind == "GELU":
                    wait_read(act, "HP", n)
                    act.activation(hp[:, n % 4, :], hp[:, n % 4, :], ACT.Gelu).then_inc(gelu_ready, 1)

        @block.vector
        def _(dve):
            links = [0]
            dve.wait_ge(gate_in, 48)
            dve.tensor_scalar(b2e_sb[:], b2e_sb[:], 2.0, None, ALU.mult).then_inc(b2_doubled, 1)

            def link(ins):
                links[0] += 1
                ins.then_inc(chain, 1)
                dve.wait_ge(chain, links[0])

            dve.memset(zeros16[:], 0.0)
            dve.memset(gmax[:], -1.0)
            dve.memset(ones_sq[:], 1.0).then_inc(ones_sq_ready, 1)
            dve.wait_ge(bias_in, 32)
            dve.tensor_scalar(b1_half[:], b1_sb[:], 0.5, None, ALU.mult).then_inc(b1_halved, 1)
            dve.wait_ge(moe_in, 32)
            for q in range(EXPERTS * P // BANK):
                cols = slice(q * BANK, (q + 1) * BANK)
                dve.tensor_copy(w3_hi[:, cols], w3_sb[:, cols]).then_inc(w3_hi_ready, 1)
                link(dve.tensor_copy(w1_hi[:, cols], w1_sb[:, cols]))
                dve.tensor_tensor(w1_lo[:, cols], w1_sb[:, cols], w1_hi[:, cols].bitcast(F32), ALU.subtract).then_inc(w1_split, 1)
            def setup_stage(d):
                if d == 0:
                    dve.wait_ge(l1_in, 96)
                    dve.wait_ge(ident_ready, 1)
                    dve.tensor_copy(ident_bf[:], ident[:])
                    dve.tensor_tensor(wc2[:], wc_sb[:], wc_sb[:], ALU.mult)
                    return dve.tensor_scalar(ysT[:], cond_sb[:], float(P) ** -0.5, None, ALU.mult)
                if d == 1:
                    dve.tensor_reduce(f_abs[:, 0:1], f1_sb[:], AX_X, ALU.add, apply_absolute_value=True)
                    return dve.tensor_tensor(ys2[:], ysT[:], ysT[:], ALU.mult)
                if d == 2:
                    return dve.tensor_reduce(f_abs[:, 1:2], f2_sb[:], AX_X, ALU.add, apply_absolute_value=True)
                if d == 3:
                    dve.wait_ge(setup_pe, 1)
                    dve.tensor_scalar(d_sum[:], y_ps[:, 0:BATCH], 1e-8, None, ALU.add)
                    return dve.tensor_scalar(f_scale[:], y_ps[:, BATCH:BATCH + 2], 1.0 / (P * HIDDEN), 1e-5, ALU.mult, ALU.max)
                if d == 4:
                    return dve.reciprocal(f_inv[:], f_scale[:])
                f2_flat = f2_q[:].rearrange("p a b -> p (a b)")
                if d == 5:
                    dve.tensor_scalar(f1_sb[:], f1_sb[:], f_inv[:, 0:1], MAGIC, ALU.mult, ALU.add)
                    return dve.tensor_scalar(f2_sb[:], f2_sb[:], f_inv[:, 1:2], MAGIC, ALU.mult, ALU.add)
                if d == 6:
                    dve.tensor_scalar(f1_sb[:], f1_sb[:], MAGIC, -1.0, ALU.subtract, ALU.max)
                    return dve.tensor_scalar(f2_sb[:], f2_sb[:], MAGIC, -1.0, ALU.subtract, ALU.max)
                if d == 7:
                    dve.tensor_scalar(f1_q[:], f1_sb[:], 1.0, None, ALU.min)
                    return dve.tensor_scalar(f2_flat, f2_sb[:], 1.0, None, ALU.min)
                if d == 8:
                    dve.wait_ge(setup_pool, 1)
                    return dve.tensor_copy(dT_rep[:].rearrange("p (t b) -> p t b", b=BATCH),
                                           dT[:].rearrange("p (o b) -> p o b", o=1).broadcast_to([P, STEPS_PER_TILE, BATCH]))
                dve.wait_ge(setup_pe, 2)
                return dve.tensor_copy(demod[:], y_ps[:, 0:P])

            def select_stage(d, n, values, width, k, sel):
                v = values[:, 0:n, 0:width]
                least = top8[:, 0:n, k - 1:k].broadcast_to([P, n, width])
                gt, eq, bf, ft = (m[:, 0:n, 0:width] for m in (above, equal, before, fits))
                if d == 0:
                    for i in range(n):
                        ins = dve.max(top8[:, i, :], values[:, i, :])
                elif d == 1:
                    dve.tensor_tensor(gt, v, least, ALU.is_gt)
                    ins = dve.tensor_tensor(eq, v, least, ALU.is_equal)
                elif d == 2:
                    ins = dve.tensor_reduce(n_above[:, 0:n], gt, AX_X, ALU.add)
                elif d == 3:
                    for i in range(n):
                        ins = dve.tensor_tensor_scan(before[:, i, 0:width], equal[:, i, 0:width], zeros16[:, 0:width],
                                                     n_above[:, i:i + 1], ALU.add, ALU.add)
                elif d == 4:
                    ins = dve.scalar_tensor_tensor(out=ft, in0=bf, scalar=float(k), in1=eq, op0=ALU.is_le, op1=ALU.mult)
                else:
                    ins = dve.tensor_tensor(sel, ft, gt, ALU.add)
                return ins

            def gate_stage(c, d):
                first, n = CHUNKS[c]
                s, m = s_gate[:, 0:n, :], masked[:, 0:n, :]
                by_group = lambda ap: ap.rearrange("p n (g e) -> p (n g) e", g=GROUPS)
                g = g_sel[:, 0:n, :].rearrange("p n (g o) -> p (n g) o", o=1).broadcast_to([P, n * GROUPS, EXPERTS // GROUPS])
                if d == 0:
                    dve.wait_ge(exp_ready, (first + n) * EXP_PARTS)
                    return dve.tensor_scalar(s, exp_neg[:, first:first + n, :], 1.0, None, ALU.add)
                if d == 1:
                    return dve.reciprocal(s, s)
                if d == 2:
                    return dve.tensor_reduce(gmax[:, 0:n, 0:GROUPS], s.rearrange("p n (g e) -> p n g e", g=GROUPS), AX_X, ALU.max)
                if d < 9:
                    return select_stage(d - 3, n, gmax, GROUPS, TOP_GROUPS, g_sel[:, 0:n, :])
                if d == 9:
                    return dve.tensor_tensor(by_group(m), by_group(s), g, ALU.mult)
                if d == 10:
                    return dve.scalar_tensor_tensor(out=by_group(m), in0=g, scalar=-1.0, in1=by_group(m),
                                                    op0=ALU.add, op1=ALU.add)
                if d < 17:
                    return select_stage(d - 11, n, masked, EXPERTS, TOP_EXPERTS, e_sel[:, 0:n, :])
                if d == 17:
                    return dve.tensor_tensor(w_raw[:, 0:n, :], e_sel[:, 0:n, :], s, ALU.mult)
                if d == 18:
                    return dve.tensor_reduce(w_sum[:, 0:n], w_raw[:, 0:n, :], AX_X, ALU.add)
                if d == 19:
                    return dve.reciprocal(w_inv[:, 0:n], w_sum[:, 0:n])
                return dve.scalar_tensor_tensor(out=we[:, first:first + n, :], in0=w_raw[:, 0:n, :], scalar=ROUTE_SCALE / 2,
                                                in1=w_inv[:, 0:n].rearrange("p (n o) -> p n o", o=1).broadcast_to([P, n, EXPERTS]),
                                                op0=ALU.mult, op1=ALU.mult)

            marks = {}

            def mark(ins, key):
                links[0] += 1
                ins.then_inc(chain, 1)
                marks[key] = links[0]

            def after(key):
                dve.wait_ge(chain, marks[key])

            for kind, n in SCHEDULE:
                if kind == "SETUP":
                    if n:
                        dve.wait_ge(setup_dve, n)
                    setup_stage(n).then_inc(setup_dve, 1)
                if kind == "SCORES_READ":
                    wait_filled(dve, "SCORES", n)
                    dve.tensor_scalar(neg_scores[:, n, :], m_ps[:, 0:EXPERTS], -1.0, None, ALU.mult).then_inc(freed[M], 1)
                if kind == "SPLIT":
                    cols = chunk_cols(n)
                    dve.wait_ge(h_ready, (CHUNKS[n][0] + CHUNKS[n][1]) * STEPS_PER_TILE)
                    link(dve.tensor_copy(hs_hi[:, cols], hs[:, cols]))
                    dve.tensor_tensor(hs_lo[:, cols], hs[:, cols], hs_hi[:, cols].bitcast(F32), ALU.subtract).then_inc(hs_split, 1)
                if kind == "GATE":
                    c, d = divmod(n, GATE_STAGES)
                    if n:
                        dve.wait_ge(gate_step, n)
                    gate_stage(c, d).then_inc(gate_step, 1)
                if kind == "WT_READ":
                    wait_filled(dve, "WT", n)
                    dve.tensor_copy(weT[:, tile_cols(n)], m_ps[0:EXPERTS, 0:P]).then_inc(freed[M], 1)
                if kind == "GATED":
                    w = chunk_of(n)[1] * P
                    if n >= H_RING:
                        dve.wait_ge(y_done, n - H_RING + 1)
                    dve.wait_ge(gate_ready, n + 1)
                    dve.scalar_tensor_tensor(out=hid[:, n % H_RING, 0:w], in0=gate_t[:, n % 4, 0:w], scalar=1.0,
                                             in1=gate_a[:, n % 4, 0:w], op0=ALU.add, op1=ALU.mult).then_inc(gated, 1)
                if kind == "HIDDEN":
                    e = n % EXPERTS
                    w = chunk_of(n)[1] * P
                    h = hid[:, n % H_RING, 0:w]
                    dve.wait_ge(gated, n + 1)
                    dve.wait_ge(b_ready, n + 1)
                    dve.scalar_tensor_tensor(out=h, in0=b_ps[n % 2][:, 0:w], scalar=b3_sb[:, e:e + 1],
                                             in1=h, op0=ALU.add, op1=ALU.mult).then_inc(hid_ready, 1)
                if kind == "FIN_READ":
                    cols = chunk_cols(n)
                    w = CHUNKS[n][1] * P
                    if n == 0:
                        dve.wait_ge(x_in, 16)
                        dve.wait_ge(xw_in, 48)
                    dve.wait_ge(chunk_y, n + 1)
                    link(dve.tensor_tensor(x1T[:, cols], y_ps[:, 0:w], xT_sb[:, cols], ALU.add))
                    dve.tensor_tensor(zT[:, cols].rearrange("p (t b) -> p t b", b=BATCH),
                                      x1T[:, cols].rearrange("p (t b) -> p t b", b=BATCH),
                                      ysT[:].rearrange("p (o b) -> p o b", o=1).broadcast_to([P, w // BATCH, BATCH]),
                                      ALU.mult).then_inc(x1_ready, 1)
                if kind == "X_READ":
                    bank = banks[bank_of("X", n)]
                    wait_filled(dve, "X", n)
                    dve.tensor_tensor(x1b[:, n, :], bank[:, 0:P], fb2_bc[:], ALU.add)
                    dve.tensor_tensor(o_sb[:, n % 2, :], bank[:, P:2 * P], demod[:], ALU.mult).then_inc(freed[bank_of("X", n)], 1)
                which = 0 if kind.endswith("1") else 1
                one = slice(2 * n + which, 2 * n + which + 1)
                if kind == "AMAX1":
                    wait_read(dve, "X", n)
                    mark(dve.tensor_reduce(amax[:, one], o_sb[:, n % 2, :], AX_X, ALU.max, apply_absolute_value=True), (kind, n))
                if kind == "AMAX2":
                    dve.wait_ge(gelu_ready, n + 1)
                    mark(dve.tensor_reduce(amax[:, one], hp[:, n % 4, :], AX_X, ALU.max, apply_absolute_value=True), (kind, n))
                if kind in ("SCALE1", "SCALE2"):
                    after((f"AMAX{which + 1}", n))
                    mark(dve.tensor_scalar(step[:, one], amax[:, one], 1e-5, 1.0 / QB, ALU.max, ALU.mult), (kind, n))
                if kind in ("RECIP1", "RECIP2"):
                    after((f"SCALE{which + 1}", n))
                    dve.tensor_scalar(deq[:, one], step[:, one], f_scale[:, which:which + 1], None, ALU.mult)
                    mark(dve.reciprocal(inv_step[:, one], step[:, one]), (kind, n))
                if kind == "ROUND1":
                    after(("RECIP1", n))
                    mark(dve.tensor_scalar(q_f[:, n % 2, :], o_sb[:, n % 2, :], inv_step[:, one], MAGIC, ALU.mult, ALU.add), (kind, n))
                if kind == "ROUND2":
                    after(("RECIP2", n))
                    mark(dve.tensor_scalar(q2_f[:, n % 2, :], hp[:, n % 4, :], inv_step[:, one], MAGIC, ALU.mult, ALU.add), (kind, n))
                if kind == "INT1":
                    after(("ROUND1", n))
                    dve.tensor_scalar(q_bf[:, n % 2, :], q_f[:, n % 2, :], MAGIC, QB, ALU.subtract, ALU.min).then_inc(q_ready, 1)
                if kind == "INT2":
                    after(("ROUND2", n))
                    dve.tensor_scalar(q2_bf[:, n % 2, :], q2_f[:, n % 2, :], MAGIC, QB, ALU.subtract, ALU.min).then_inc(q2_ready, 1)
                if kind == "Q_READ":
                    wait_filled(dve, "Q", n)
                    dve.tensor_copy(qT[:, n % 2, :], m_ps[:, 0:P // 2].bitcast(BF16)).then_inc(freed[M], 1)
                if kind == "HP_READ":
                    wait_filled(dve, "HP", n)
                    b = bank_of("HP", n)
                    dve.scalar_tensor_tensor(out=hp[:, n % 4, :], in0=banks[b][:], scalar=deq[:, 2 * n:2 * n + 1],
                                             in1=fb1_bc[:], op0=ALU.mult, op1=ALU.add).then_inc(freed[b], 1)
                if kind == "OUT_READ":
                    b = bank_of("OUT", n)
                    wait_filled(dve, "OUT", n)
                    dve.scalar_tensor_tensor(out=out_sb[:, n, :], in0=banks[b][:, 0:P], scalar=deq[:, 2 * n + 1:2 * n + 2],
                                             in1=x1b[:, n, :], op0=ALU.mult, op1=ALU.add).then_inc(freed[b], 1)

        @block.tensor
        def _(pe):
            pe.wait_ge(xw_in, 48)
            pe.wait_ge(ones_ready, 1)

            def rnn_inputs(i):
                ps = rnn_bank(i * P, P)
                pe.matmul(ps, wx_sb[:], xT_sb[:, tile_cols(i)], start=(i in (0, 1, BANK // P)), stop=False,
                          skip_group_check=True)
                pe.matmul(ps, bh_sb[:], ones_row[:, 0:P], start=False, stop=False, skip_group_check=True)

            rnn_inputs(0)

            def products(ps, w32, hi, lo, j):
                c, e = divmod(j, EXPERTS)
                cols, ex = chunk_cols(c), expert_cols(e)
                w = CHUNKS[c][1] * P
                if CHUNKS[c][1] == 1:
                    return pe.matmul(ps[:, 0:w], w32[:, ex], hs[:, cols], start=True, stop=True)
                pe.matmul(ps[:, 0:w], lo[:, ex], hs_hi[:, cols], start=True, stop=False)
                pe.matmul(ps[:, 0:w], hi[:, ex], hs_lo[:, cols], start=False, stop=False)
                return pe.matmul(ps[:, 0:w], hi[:, ex], hs_hi[:, cols], start=False, stop=True)

            for kind, n in SCHEDULE:
                if kind == "RNN":
                    if n == 0:
                        pe.wait_ge(rnn_in, 32)
                    else:
                        pe.wait_ge(h_ready, n)
                    prev = h0_sb[:] if n == 0 else hs[:, (n - 1) * BATCH:n * BATCH]
                    pe.matmul(rnn_bank(n * BATCH, BATCH), wh_sb[:], prev, start=False, stop=True,
                              skip_group_check=True).then_inc(z_ready, 1)
                    if n == 2:
                        pe.wait_ge(x_in, 16)
                    if 2 <= n < 2 + TILES - 1:
                        rnn_inputs(n - 1)
                if (kind, n) == ("SETUP", 2):
                    pe.wait_ge(ones_sq_ready, 1)
                    pe.wait_ge(setup_dve, 3)
                    pe.matmul(y_ps[:, 0:BATCH], wc2[:], ys2[:], start=True, stop=True, skip_group_check=True)
                    pe.matmul(y_ps[:, BATCH:BATCH + 2], ones_sq[:], f_abs[:], start=True, stop=True,
                              skip_group_check=True).then_inc(setup_pe, 1)
                if (kind, n) == ("SETUP", 8):
                    pe.wait_ge(setup_dve, 9)
                    pe.transpose(y_ps[:, 0:P], dT_rep[:], ident[:]).then_inc(setup_pe, 1)
                if kind == "SCORES":
                    if n == 0:
                        pe.wait_ge(gate_in, 48)
                    if n == TILES - 1:
                        pe.wait_ge(h_ready, STEPS)
                    wait_free(pe, kind, n)
                    pe.matmul(m_ps[:, 0:EXPERTS], hs[:, tile_cols(n)], wg_sb[:], start=True, stop=True).then_inc(filled[M], 1)
                if kind == "WT":
                    c = chunk_with(n)
                    pe.wait_ge(gate_step, (c + 1) * GATE_STAGES)
                    wait_free(pe, kind, n)
                    pe.transpose(m_ps[0:EXPERTS, 0:P], we[:, n, :], ident[:]).then_inc(filled[M], 1)
                if kind == "A":
                    c = n // EXPERTS
                    if n == 0:
                        pe.wait_ge(moe_in, 32)
                    if CHUNKS[c][1] > 1:
                        first_big = min(k for k, ch in enumerate(CHUNKS) if ch[1] > 1)
                        pe.wait_ge(w1_split, EXPERTS * P // BANK)
                        pe.wait_ge(w3_split, EXPERTS * P // BANK)
                        pe.wait_ge(hs_split, c - first_big + 1)
                    if n >= 2:
                        pe.wait_ge(gate_ready, n - 1)
                    products(a_ps[n % 2], w1_sb, w1_hi, w1_lo, n).then_inc(a_ready, 1)
                if kind == "B":
                    if n >= 2:
                        pe.wait_ge(hid_ready, n - 1)
                    products(b_ps[n % 2], w3_sb, w3_hi, w3_lo, n).then_inc(b_ready, 1)
                if kind == "Y":
                    c, e = divmod(n, EXPERTS)
                    w = chunk_of(n)[1] * P
                    if n == 0:
                        pe.wait_ge(setup_dve, SETUP_STAGES)
                    if e == 0 and c:
                        pe.wait_ge(x1_ready, c)
                    pe.wait_ge(hid_weighted, n + 1)
                    pe.matmul(y_ps[:, 0:w], w2_sb[:, expert_cols(e)], hid[:, n % H_RING, 0:w],
                              start=(e == 0), stop=False).then_inc(y_done, 1)
                if kind == "FIN":
                    pe.wait_ge(b2_doubled, 1)
                    wait_read(pe, "WT", CHUNKS[n][0] + CHUNKS[n][1] - 1)
                    pe.matmul(y_ps[:, 0:CHUNKS[n][1] * P], b2e_sb[:], weT[:, chunk_cols(n)],
                              start=False, stop=True).then_inc(chunk_y, 1)
                if kind == "X":
                    bank = banks[bank_of(kind, n)]
                    c = chunk_with(n)
                    pe.wait_ge(x1_ready, c + 1)
                    wait_free(pe, kind, n)
                    pe.transpose(bank[:, 0:P], x1T[:, tile_cols(n)], ident[:])
                    pe.matmul(bank[:, P:2 * P], zT[:, tile_cols(n)], wc_sb[:], start=True, stop=True,
                              skip_group_check=True).then_inc(filled[bank_of(kind, n)], 1)
                if kind == "Q":
                    pe.wait_ge(q_ready, n + 1)
                    wait_free(pe, kind, n)
                    pe.transpose(m_ps[:, 0:P // 2].bitcast(BF16), q_bf[:, n % 2, :], ident_bf[:]).then_inc(filled[M], 1)
                if kind == "HP":
                    b = bank_of(kind, n)
                    wait_read(pe, "Q", n)
                    wait_free(pe, kind, n)
                    pe.matmul(banks[b][:], qT[:, n % 2, :], f1_q[:], start=True, stop=True).then_inc(filled[b], 1)
                if kind == "T2":
                    b = bank_of(kind, n)
                    pe.wait_ge(q2_ready, n + 1)
                    wait_free(pe, kind, n)
                    for k in range(HB):
                        last = pe.transpose(banks[b][:, k * P // 2:(k + 1) * P // 2].bitcast(BF16),
                                            q2_bf[:, n % 2, k * P:(k + 1) * P], ident_bf[:])
                    last.then_inc(filled[b], 1)
                if kind == "OUT":
                    b = bank_of(kind, n)
                    wait_read(pe, "T2", n)
                    wait_free(pe, kind, n)
                    for k in range(HB):
                        last = pe.matmul(banks[b][:, 0:P], q2T[:, n % 2, k * P:(k + 1) * P], f2_q[:, k, :],
                                         start=(k == 0), stop=(k == HB - 1))
                    last.then_inc(filled[b], 1)


def kernel(x, cond_1024, L0_cond_Wx, L0_cond_Wh, L0_cond_b, L0_ffn_Wg, L0_ffn_W1, L0_ffn_b1,
           L0_ffn_W2, L0_ffn_b2, L0_ffn_W3, L0_ffn_b3, L1_cond_weight, L1_ffn_W1, L1_ffn_b1,
           L1_ffn_W2, L1_ffn_b2):
    import numpy as np
    import concourse.bacc as bacc
    from concourse.bass_utils import run_bass_kernel_spmd

    def lay(a, *shape):
        return np.ascontiguousarray(a).reshape(shape)

    x = np.asarray(x)
    by_step = x.transpose(1, 0, 2).reshape(TOKENS, P)
    cond = np.asarray(cond_1024)
    experts = lambda w: lay(np.asarray(w).transpose(2, 0, 1), P, EXPERTS * P)
    arrays = {
        "xT": lay(by_step.T, P, TOKENS),
        "h0T": lay(cond.T, P, BATCH),
        "Wx": lay(L0_cond_Wx, P, P),
        "Wh": lay(L0_cond_Wh, P, P),
        "bh": lay(L0_cond_b, 1, P),
        "WgT": lay(np.asarray(L0_ffn_Wg).T, P, EXPERTS),
        "W1T": experts(L0_ffn_W1),
        "W3T": experts(L0_ffn_W3),
        "W2T": experts(L0_ffn_W2),
        "b1T": lay(np.asarray(L0_ffn_b1).T, P, EXPERTS),
        "b3T": lay(np.asarray(L0_ffn_b3).T, P, EXPERTS),
        "b2e": lay(L0_ffn_b2, EXPERTS, P),
        "condT": lay(cond.T, P, BATCH),
        "Wc": lay(L1_cond_weight, P, P),
        "F1T": lay(np.asarray(L1_ffn_W1).T, P, HIDDEN),
        "F2T": lay(np.asarray(L1_ffn_W2).T.reshape(HB, P, P).transpose(1, 0, 2), P, HIDDEN),
        "fb1": lay(L1_ffn_b1, 1, HIDDEN),
        "fb2": lay(L1_ffn_b2, 1, P),
    }
    nc = bacc.Bacc("TRN2", target_bir_lowering=False, num_devices=1)
    aps = {name: nc.dram_tensor(name, a.shape, F32, kind="ExternalInput").ap() for name, a in arrays.items()}
    we_dram = nc.dram_tensor("we_dram", (EXPERTS, TOKENS), F32, kind="Internal").ap()
    out = nc.dram_tensor("out", (TILES, P, P), F32, kind="ExternalOutput").ap()
    adaln_ffn(nc, None, we_dram=we_dram, out=out, **aps)
    r = run_bass_kernel_spmd(nc, [arrays], core_ids=[0])
    y = r.results[0]["out"]
    return np.ascontiguousarray(y.reshape(STEPS, BATCH, P).transpose(1, 0, 2))
```

```python
import math
from contextlib import ExitStack

import concourse.bass as bass
from concourse import mybir

ALU = mybir.AluOpType
ACT = mybir.ActivationFunctionType
AX_X = mybir.AxisListType.X
F32 = mybir.dt.float32
F32R = mybir.dt.float32r
BF16 = mybir.dt.bfloat16

P = 128
BATCH = 8
STEPS = 128
TOKENS = BATCH * STEPS
TILES = TOKENS // P
STEPS_PER_TILE = P // BATCH
BANK = 512
EXPERTS = 16
GROUPS = 4
TOP_GROUPS = 2
TOP_EXPERTS = 4
ROUTE_SCALE = 2.5
QB = 127.0
HIDDEN = 512
HB = HIDDEN // P
MAGIC = 1.5 * 2.0 ** 23
E_CONST = 2.718281828459045

CHUNKS = [(0, 1), (1, 1), (2, 2), (4, 2), (6, 2)]
LAST_CHUNK = len(CHUNKS) - 1
JOBS = len(CHUNKS) * EXPERTS
H_RING = 32
GATE_STAGES = 21
EXP_PARTS = 4
SETUP_STAGES = 10

SETUP_AT = 13.47
CHUNK_GAP = 0.5
SHORT_JOB_TIME, LONG_JOB_TIME = 1.67, 2.45
TAIL_JOB_TIME = 1.67
ACT_GAP = 0.9
GATED_GAP, HIDDEN_GAP = 1.65, 0.61
W_LAG, TAIL_W_LAG = 5.86, 5.0
Y_LAG = 3.59
EXP_AT = 1.38
EXP_TIME, TAIL_EXP_TIME = 1.35, 1.35
GATE_AT, TAIL_GATE_AT = 2.21, 2.89
GATE_TIME, TAIL_GATE_TIME = 0.52, 0.91
WEIGHTS_AT, TAIL_WEIGHTS_AT = 10.5, 2.26
FIN_LAG = 1.6
TILE_LAG, TAIL_TILE_LAG = 6.82, 2.16
L1_SCALE, TAIL_L1_SCALE = 1.39, 2.27
ROUND_ACT_FROM = 4
PASSES = {1: 1, 2: 3}
MAX_PASSES = 3

START_KEEPS = 22
KEEP_TIME = 107
RNN_INPUTS_TIME = 427
EARLY_PE_BUSY, PE_BUSY = 540, 400
L1_TIMES = {"X": 0.0, "X_READ": 1.0, "AMAX1": 1.6, "SCALE1": 2.2, "RECIP1": 2.7, "ROUND1": 3.3,
            "INT1": 3.9, "Q": 5.5, "Q_READ": 6.5, "HP": 8.0, "HP_READ": 9.0, "GELU": 10.0,
            "AMAX2": 11.5, "SCALE2": 12.3, "RECIP2": 12.8, "ROUND2": 13.4, "INT2": 14.0,
            "T2": 16.0, "T2_READ": 16.5, "OUT": 18.5, "OUT_READ": 19.5}


def chunk_of(j):
    return CHUNKS[j // EXPERTS]


def chunk_with(i):
    return next(c for c, (first, n) in enumerate(CHUNKS) if first <= i < first + n)


def pe_time(kind, n):
    if kind in ("A", "B"):
        return 213 if chunk_of(n // MAX_PASSES)[1] == 1 else 107
    return {"Y": 213, "SCORES": 107, "WT": 107, "X": 427, "Q": 56, "HP": 213, "T2": 224, "OUT": 224}.get(kind, 0)


def build_schedule():
    timed = []

    def at(time, kind, n):
        timed.append((time, len(timed), kind, n))

    for t in range(STEPS):
        at(t, "RNN", t)
    for d in range(SETUP_STAGES):
        at(SETUP_AT + d, "SETUP", d)
    exp_free = 0.0
    product_time = down_time = 0.0
    for c, (first, n) in enumerate(CHUNKS):
        for i in range(first, first + n):
            done = (i + 1) * STEPS_PER_TILE
            at(done + 0.1, "SCORES", i)
            at(done + 1.2, "SCORES_READ", i)
            exp_free = max(exp_free, done + EXP_AT)
            for q in range(EXP_PARTS):
                at(exp_free, "EXP", i * EXP_PARTS + q)
                exp_free += EXP_TIME if c < LAST_CHUNK else TAIL_EXP_TIME
        done = (first + n) * STEPS_PER_TILE
        if n > 1:
            at(done + 0.2, "SPLIT", c)
        gate = exp_free + (GATE_AT if c < LAST_CHUNK else TAIL_GATE_AT)
        gate_time = GATE_TIME if c < LAST_CHUNK else TAIL_GATE_TIME
        for d in range(GATE_STAGES):
            at(gate + d * gate_time, "GATE", c * GATE_STAGES + d)
        gate += GATE_STAGES * gate_time + 1.0
        for i in range(first, first + n):
            at(gate, "WT", i)
            at(gate + 1.0, "WT_READ", i)
            gate += 1.5
        at(gate, "WB", c)
        weighted = gate + (WEIGHTS_AT if c < LAST_CHUNK else TAIL_WEIGHTS_AT)
        product_time = max(product_time, done + CHUNK_GAP)
        for e in range(EXPERTS):
            j = c * EXPERTS + e
            long = (SHORT_JOB_TIME if n == 1 else LONG_JOB_TIME) if product_time < STEPS else TAIL_JOB_TIME
            for p in range(PASSES[n]):
                at(product_time + p * 0.3 * long / PASSES[n], "A", j * MAX_PASSES + p)
                at(product_time + (p / PASSES[n] + 1) * 0.3 * long, "B", j * MAX_PASSES + p)
            at(product_time + 0.3 * long + 0.02, "TANH", j)
            at(product_time + 0.3 * long + ACT_GAP, "LINEAR", j)
            at(product_time + 0.3 * long + ACT_GAP + GATED_GAP, "GATED", j)
            at(product_time + 0.3 * long + ACT_GAP + GATED_GAP + HIDDEN_GAP, "HIDDEN", j)
            down_time = max(down_time, product_time + (W_LAG if product_time < STEPS else TAIL_W_LAG), weighted)
            at(down_time, "W", j)
            for p in range(n):
                at(down_time + Y_LAG + 0.2 * long * p, "Y", j * 2 + p)
            product_time += long
            down_time += long
        fin = down_time + Y_LAG
        at(fin, "FIN", c)
        at(fin + 0.8, "FIN_READ", c)
        start = max(fin + FIN_LAG, STEPS / 2 + 1)
        lag, scale = (TILE_LAG, L1_SCALE) if c < LAST_CHUNK else (TAIL_TILE_LAG, TAIL_L1_SCALE)
        for m in range(n):
            for kind, offset in L1_TIMES.items():
                at(start + lag * m + scale * offset, kind, first + m)
    busy = [0.0] * STEPS
    for i in range(1, TILES):
        busy[i + 1] += RNN_INPUTS_TIME
    for time, _, kind, n in timed:
        if time < STEPS:
            busy[int(time)] += pe_time(kind, n)
    for t in range(STEPS):
        for k in range(math.ceil(((PE_BUSY if t >= STEPS_PER_TILE else EARLY_PE_BUSY) - busy[t]) / KEEP_TIME)):
            at(t + 0.15 + 0.1 * k, "KEEP", 0)
    order = [(kind, n) for _, _, kind, n in sorted(timed)]
    job = 0
    for at_, (kind, n) in enumerate(order):
        if kind == "A":
            job = n // MAX_PASSES + 1
        if kind == "KEEP":
            order[at_] = (kind, job)
    return order


SCHEDULE = build_schedule()

M, R0, R1 = range(3)


def bank_of(kind, i):
    if kind in ("SCORES", "WT", "Q"):
        return M
    if kind in ("X", "HP"):
        return R1 if i == TILES - 1 else R0
    return R1 if i == TILES - 1 else M


def bank_uses():
    count, place = [0, 0, 0], {}
    for kind, i in SCHEDULE:
        if kind in ("SCORES", "WT", "X", "Q", "HP", "T2", "OUT"):
            b = bank_of(kind, i)
            place[(kind, i)] = (b, count[b])
            count[b] += 1
    return place


USES = bank_uses()


def adaln_ffn(nc, xT, h0T, Wx, Wh, bh, WgT, W1T, W3T, W2T, b1T, b3T, b2e,
              condT, Wc, F1T, F2T, fb1, fb2, we_dram, out):
    with ExitStack() as ctx:
        def sb(name, shape, dt=F32):
            return ctx.enter_context(nc.sbuf_tensor(name, shape, dt))

        def psum(name):
            return ctx.enter_context(nc.psum_tensor(name, [P, BANK], F32))

        def sem(name):
            return ctx.enter_context(nc.semaphore(name))

        xT_sb = sb("xT_sb", [P, TOKENS])
        warm_sb = sb("warm_sb", [P, 256], BF16)
        h0_sb = sb("h0_sb", [P, BATCH])
        wx_sb, wh_sb = sb("wx_sb", [P, P]), sb("wh_sb", [P, P])
        bh_sb = sb("bh_sb", [1, P])
        ones_row = sb("ones_row", [1, BANK])
        hs = sb("hs", [P, TOKENS])
        hs_hi, hs_lo = sb("hs_hi", [P, TOKENS], F32R), sb("hs_lo", [P, TOKENS], F32R)
        w1_sb, w3_sb = sb("w1_sb", [P, EXPERTS * P]), sb("w3_sb", [P, EXPERTS * P])
        w2_sb = sb("w2_sb", [P, EXPERTS * P])
        w1_hi, w1_lo = sb("w1_hi", [P, EXPERTS * P], F32R), sb("w1_lo", [P, EXPERTS * P], F32R)
        w3_hi, w3_lo = sb("w3_hi", [P, EXPERTS * P], F32R), sb("w3_lo", [P, EXPERTS * P], F32R)
        b1_sb, b1_half, b3_sb = sb("b1_sb", [P, EXPERTS]), sb("b1_half", [P, EXPERTS]), sb("b3_sb", [P, EXPERTS])
        b2e_sb = sb("b2e_sb", [EXPERTS, P])
        wg_sb = sb("wg_sb", [P, EXPERTS])
        gate_t = sb("gate_t", [P, 4, 256])
        gate_a = sb("gate_a", [P, 4, 256])
        hid = sb("hid", [P, H_RING, 256])
        we_bc = sb("we_bc", [P, 2, EXPERTS, 256])
        weT = sb("weT", [EXPERTS, TOKENS])
        magic = sb("magic", [P, 1])
        e_const = sb("e_const", [P, EXPERTS])
        neg_scores, exp_neg = sb("neg_scores", [P, TILES, EXPERTS]), sb("exp_neg", [P, TILES, EXPERTS])
        s_gate, masked, w_raw = (sb(n, [P, 2, EXPERTS]) for n in ("s_gate", "masked", "w_raw"))
        gmax, top8 = sb("gmax", [P, 2, 8]), sb("top8", [P, 2, 8])
        above, equal, before, fits = (sb(n, [P, 2, EXPERTS]) for n in ("above", "equal", "before", "fits"))
        g_sel, e_sel = sb("g_sel", [P, 2, GROUPS]), sb("e_sel", [P, 2, EXPERTS])
        n_above, w_sum, w_inv = (sb(n, [P, 2]) for n in ("n_above", "w_sum", "w_inv"))
        zeros16 = sb("zeros16", [P, EXPERTS])
        we = sb("we", [P, TILES, EXPERTS])
        x1T, zT = sb("x1T", [P, TOKENS]), sb("zT", [P, TOKENS])
        cond_sb, ysT, ys2 = sb("cond_sb", [P, BATCH]), sb("ysT", [P, BATCH]), sb("ys2", [P, BATCH])
        wc_sb, wc2 = sb("wc_sb", [P, P]), sb("wc2", [P, P])
        neg_half, d_sum, dT = sb("neg_half", [P, BATCH]), sb("d_sum", [P, BATCH]), sb("dT", [P, BATCH])
        dT_rep = sb("dT_rep", [P, P])
        demod = sb("demod", [P, P])
        f1_sb, f2_sb = sb("f1_sb", [P, HIDDEN]), sb("f2_sb", [P, HIDDEN])
        f1_q, f2_q = sb("f1_q", [P, HIDDEN], BF16), sb("f2_q", [P, HB, P], BF16)
        f_abs, f_scale, f_inv = (sb(n, [P, 2]) for n in ("f_abs", "f_scale", "f_inv"))
        fb1_bc, fb2_bc = sb("fb1_bc", [P, HIDDEN]), sb("fb2_bc", [P, P])
        ident, ident_bf, ones_sq = sb("ident", [P, P]), sb("ident_bf", [P, P], BF16), sb("ones_sq", [P, P])
        x1b = sb("x1b", [P, TILES, P])
        o_sb, q_f = sb("o_sb", [P, 2, P]), sb("q_f", [P, 2, P])
        q_bf, qT = sb("q_bf", [P, 2, P], BF16), sb("qT", [P, 2, P], BF16)
        amax, step, inv_step, deq = (sb(n, [P, 2 * TILES]) for n in ("amax", "step", "inv_step", "deq"))
        hp = sb("hp", [P, 4, HIDDEN])
        q2_f, q2_bf, q2T = sb("q2_f", [P, 2, HIDDEN]), sb("q2_bf", [P, 2, HIDDEN], BF16), sb("q2T", [P, 2, HIDDEN], BF16)
        out_sb = sb("out_sb", [P, TILES, P])

        rnn_ps = [psum("rnn0"), psum("rnn1")]
        a_ps, b_ps = [psum("a0"), psum("a1")], [psum("b0"), psum("b1")]
        y_ps, m_ps = psum("y_ps"), psum("m_ps")
        banks = [m_ps, rnn_ps[0], rnn_ps[1]]

        rnn_in, xw_in, x_in, moe_in, gate_in, down_in, l1_in, bias_in = (sem(n) for n in (
            "rnn_in", "xw_in", "x_in", "moe_in", "gate_in", "down_in", "l1_in", "bias_in"))
        ident_zero, ident_ready, ones_sq_ready, ones_ready, const_ready = (sem(n) for n in (
            "ident_zero", "ident_ready", "ones_sq_ready", "ones_ready", "const_ready"))
        warm_ready = sem("warm_ready")
        z_ready, h_ready = sem("z_ready"), sem("h_ready")
        w1_split, w3_hi_ready, w3_split, hs_split = (sem(n) for n in ("w1_split", "w3_hi_ready", "w3_split", "hs_split"))
        b1_halved, b2_doubled = sem("b1_halved"), sem("b2_doubled")
        a_ready, b_ready, gate_ready, gated = (sem(n) for n in ("a_ready", "b_ready", "gate_ready", "gated"))
        hid_ready, hid_weighted, y_done = (sem(n) for n in ("hid_ready", "hid_weighted", "y_done"))
        chunk_y, x1_ready = sem("chunk_y"), sem("x1_ready")
        exp_ready = sem("exp_ready")
        gate_step = sem("gate_step")
        we_stored, we_loaded = sem("we_stored"), [[sem(f"we_loaded{slot}_{q}") for q in range(4)] for slot in range(2)]
        filled = [sem(f"filled{n}") for n in range(3)]
        freed = [sem(f"freed{n}") for n in range(3)]
        setup_pe, setup_dve, setup_pool = sem("setup_pe"), sem("setup_dve"), sem("setup_pool")
        q_ready, gelu_ready = sem("q_ready"), sem("gelu_ready")
        magic_ready = sem("magic_ready")
        inv_ready, act_rounded = sem("inv_ready"), sem("act_rounded")
        q2_ready, stored = sem("q2_ready"), sem("stored")
        chain = sem("chain")

        def wait_filled(eng, kind, i):
            b, n = USES[(kind, i)]
            eng.wait_ge(filled[b], n + 1)

        def wait_free(eng, kind, i):
            b, n = USES[(kind, i)]
            if n:
                eng.wait_ge(freed[b], n)

        def wait_read(eng, kind, i):
            b, n = USES[(kind, i)]
            eng.wait_ge(freed[b], n + 1)

        def rnn_bank(token, n):
            if token < P:
                return m_ps[:, token:token + n]
            bank, at = divmod(token, BANK)
            return rnn_ps[bank][:, at:at + n]

        def tile_cols(i):
            return slice(i * P, (i + 1) * P)

        def chunk_cols(c):
            first, n = CHUNKS[c]
            return slice(first * P, (first + n) * P)

        def expert_cols(e):
            return slice(e * P, (e + 1) * P)

        block = ctx.enter_context(nc.Block())

        @block.sync
        def _(sp):
            sp.dma_start(xT_sb[:, 0:P], xT[:, 0:P]).then_inc(xw_in, 16)
            sp.dma_start(wx_sb[:], Wx).then_inc(xw_in, 16)
            sp.dma_start(xT_sb[:, P:TOKENS], xT[:, P:TOKENS]).then_inc(x_in, 16)
            sp.dma_start(w1_sb[:], W1T).then_inc(moe_in, 16)
            sp.dma_start(w3_sb[:], W3T).then_inc(moe_in, 16)
            sp.dma_start(b1_sb[:], b1T).then_inc(bias_in, 16)
            sp.dma_start(b3_sb[:], b3T).then_inc(bias_in, 16)
            sp.dma_start(wg_sb[:], WgT).then_inc(gate_in, 16)
            sp.dma_start(cond_sb[:], condT).then_inc(l1_in, 16)
            sp.dma_start(wc_sb[:], Wc).then_inc(l1_in, 16)
            sp.dma_start(f1_sb[:], F1T).then_inc(l1_in, 16)
            sp.dma_start(f2_sb[:], F2T).then_inc(l1_in, 16)
            sp.dma_start(fb1_bc[:], fb1.broadcast_to([P, HIDDEN])).then_inc(l1_in, 16)
            sp.dma_start(fb2_bc[:], fb2.broadcast_to([P, P])).then_inc(l1_in, 16)
            sp.dma_start(b2e_sb[:], b2e).then_inc(down_in, 16)
            sp.dma_start(w2_sb[:], W2T).then_inc(down_in, 16)
            for kind, n in SCHEDULE:
                if kind == "WB":
                    first, k = CHUNKS[n]
                    cols = chunk_cols(n)
                    wait_read(sp, "WT", first + k - 1)
                    sp.dma_start(we_dram[:, cols], weT[:, cols]).then_inc(we_stored, 16)
                    sp.wait_ge(we_stored, 16 * (n + 1))
                    if n >= 2:
                        sp.wait_ge(hid_weighted, EXPERTS * (n - 1))
                    for q in range(4):
                        sp.dma_start(we_bc[:, n % 2, 4 * q:4 * q + 4, 0:k * P],
                                     we_dram[4 * q:4 * q + 4, cols].rearrange("(o e) t -> o e t", o=1)
                                     .broadcast_to([P, 4, k * P])).then_inc(we_loaded[n % 2][q], 16)
                if kind == "OUT":
                    wait_read(sp, "OUT", n)
                    sp.dma_start(out[n], out_sb[:, n, :]).then_inc(stored, 16)
            sp.wait_ge(stored, 16 * TILES)

        @block.gpsimd
        def _(pool):
            pool.memset(warm_sb[:], 0.0).then_inc(warm_ready, 1)
            pool.memset(ones_row[:], 1.0).then_inc(ones_ready, 1)
            pool.memset(ident[:], 0.0).then_inc(ident_zero, 1)
            pool.wait_ge(ident_zero, 1)
            pool.affine_select(out=ident[:], in_=ident[:], compare_op=ALU.not_equal, fill=1.0,
                               base=0, pattern=[[-1, P]], channel_multiplier=1).then_inc(ident_ready, 1)
            pool.memset(magic[:], MAGIC).then_inc(magic_ready, 1)
            pool.memset(e_const[:], E_CONST).then_inc(const_ready, 1)
            pool.memset(neg_half[:], -0.5).then_inc(const_ready, 1)
            pool.wait_ge(const_ready, 2)
            for q in range(EXPERTS * P // BANK):
                cols = slice(q * BANK, (q + 1) * BANK)
                pool.wait_ge(w3_hi_ready, q + 1)
                pool.tensor_tensor(w3_lo[:, cols], w3_sb[:, cols], w3_hi[:, cols].bitcast(F32), ALU.subtract).then_inc(w3_split, 1)
            for kind, n in SCHEDULE:
                if (kind, n) == ("SETUP", 3):
                    pool.wait_ge(setup_dve, 4)
                    pool.tensor_tensor(dT[:], d_sum[:], neg_half[:], ALU.pow).then_inc(setup_pool, 1)
                if kind == "EXP":
                    i, q = divmod(n, EXP_PARTS)
                    part = slice(q * EXPERTS // EXP_PARTS, (q + 1) * EXPERTS // EXP_PARTS)
                    wait_read(pool, "SCORES", i)
                    pool.tensor_tensor(exp_neg[:, i, part], e_const[:, part], neg_scores[:, i, part],
                                       ALU.pow).then_inc(exp_ready, 1)
                if kind == "W":
                    c, e = divmod(n, EXPERTS)
                    w = chunk_of(n)[1] * P
                    pool.wait_ge(hid_ready, n + 1)
                    pool.wait_ge(we_loaded[c % 2][e // 4], 16 * (c // 2 + 1))
                    pool.tensor_tensor(hid[:, n % H_RING, 0:w], hid[:, n % H_RING, 0:w],
                                       we_bc[:, c % 2, e, 0:w], ALU.mult).then_inc(hid_weighted, 1)

        @block.scalar
        def _(act):
            act.dma_start(bh_sb[:], bh).then_inc(xw_in, 16)
            act.dma_start(h0_sb[:], h0T).then_inc(rnn_in, 16)
            act.dma_start(wh_sb[:], Wh).then_inc(rnn_in, 16)
            for kind, n in SCHEDULE:
                if kind == "RNN":
                    cols = slice(n * BATCH, (n + 1) * BATCH)
                    act.wait_ge(z_ready, n + 1)
                    act.activation(hs[:, cols], rnn_bank(n * BATCH, BATCH), ACT.Tanh).then_inc(h_ready, 1)
                if kind == "TANH":
                    e = n % EXPERTS
                    w = chunk_of(n)[1] * P
                    if n == 0:
                        act.wait_ge(b1_halved, 1)
                    if n >= 4:
                        act.wait_ge(gated, n - 3)
                    act.wait_ge(a_ready, n + 1)
                    act.activation(gate_t[:, n % 4, 0:w], a_ps[n % 2][:, 0:w], ACT.Tanh,
                                   bias=b1_half[:, e:e + 1], scale=0.5)
                if kind == "LINEAR":
                    e = n % EXPERTS
                    w = chunk_of(n)[1] * P
                    act.wait_ge(a_ready, n + 1)
                    act.activation(gate_a[:, n % 4, 0:w], a_ps[n % 2][:, 0:w], ACT.Identity,
                                   bias=b1_sb[:, e:e + 1]).then_inc(gate_ready, 1)
                if kind == "T2_READ":
                    b = bank_of("T2", n)
                    wait_filled(act, "T2", n)
                    act.activation(q2T[:, n % 2, :], banks[b][:, 0:HIDDEN // 2].bitcast(BF16), ACT.Copy).then_inc(freed[b], 1)
                if kind == "ROUND2" and n >= ROUND_ACT_FROM:
                    if n == ROUND_ACT_FROM:
                        act.wait_ge(magic_ready, 1)
                    act.wait_ge(inv_ready, n - ROUND_ACT_FROM + 1)
                    act.activation(q2_f[:, n % 2, :], hp[:, n % 4, :], ACT.Identity, bias=magic[:],
                                   scale=inv_step[:, 2 * n + 1:2 * n + 2]).then_inc(act_rounded, 1)
                if kind == "GELU":
                    wait_read(act, "HP", n)
                    act.activation(hp[:, n % 4, :], hp[:, n % 4, :], ACT.Gelu).then_inc(gelu_ready, 1)

        @block.vector
        def _(dve):
            links = [0]

            def link(ins):
                links[0] += 1
                ins.then_inc(chain, 1)
                dve.wait_ge(chain, links[0])

            dve.memset(zeros16[:], 0.0)
            dve.memset(gmax[:], -1.0)
            dve.memset(ones_sq[:], 1.0).then_inc(ones_sq_ready, 1)
            dve.wait_ge(bias_in, 32)
            dve.tensor_scalar(b1_half[:], b1_sb[:], 0.5, None, ALU.mult).then_inc(b1_halved, 1)
            dve.wait_ge(moe_in, 32)
            for q in range(EXPERTS * P // BANK):
                cols = slice(q * BANK, (q + 1) * BANK)
                dve.tensor_copy(w3_hi[:, cols], w3_sb[:, cols]).then_inc(w3_hi_ready, 1)
                link(dve.tensor_copy(w1_hi[:, cols], w1_sb[:, cols]))
                dve.tensor_tensor(w1_lo[:, cols], w1_sb[:, cols], w1_hi[:, cols].bitcast(F32), ALU.subtract).then_inc(w1_split, 1)
            def setup_stage(d):
                if d == 0:
                    dve.wait_ge(l1_in, 96)
                    dve.wait_ge(ident_ready, 1)
                    dve.tensor_copy(ident_bf[:], ident[:])
                    dve.tensor_tensor(wc2[:], wc_sb[:], wc_sb[:], ALU.mult)
                    return dve.tensor_scalar(ysT[:], cond_sb[:], float(P) ** -0.5, None, ALU.mult)
                if d == 1:
                    dve.tensor_reduce(f_abs[:, 0:1], f1_sb[:], AX_X, ALU.add, apply_absolute_value=True)
                    return dve.tensor_tensor(ys2[:], ysT[:], ysT[:], ALU.mult)
                if d == 2:
                    return dve.tensor_reduce(f_abs[:, 1:2], f2_sb[:], AX_X, ALU.add, apply_absolute_value=True)
                if d == 3:
                    dve.wait_ge(setup_pe, 1)
                    dve.tensor_scalar(d_sum[:], y_ps[:, 0:BATCH], 1e-8, None, ALU.add)
                    return dve.tensor_scalar(f_scale[:], y_ps[:, BATCH:BATCH + 2], 1.0 / (P * HIDDEN), 1e-5, ALU.mult, ALU.max)
                if d == 4:
                    return dve.reciprocal(f_inv[:], f_scale[:])
                f2_flat = f2_q[:].rearrange("p a b -> p (a b)")
                if d == 5:
                    dve.tensor_scalar(f1_sb[:], f1_sb[:], f_inv[:, 0:1], MAGIC, ALU.mult, ALU.add)
                    return dve.tensor_scalar(f2_sb[:], f2_sb[:], f_inv[:, 1:2], MAGIC, ALU.mult, ALU.add)
                if d == 6:
                    dve.tensor_scalar(f1_sb[:], f1_sb[:], MAGIC, -1.0, ALU.subtract, ALU.max)
                    return dve.tensor_scalar(f2_sb[:], f2_sb[:], MAGIC, -1.0, ALU.subtract, ALU.max)
                if d == 7:
                    dve.tensor_scalar(f1_q[:], f1_sb[:], 1.0, None, ALU.min)
                    return dve.tensor_scalar(f2_flat, f2_sb[:], 1.0, None, ALU.min)
                if d == 8:
                    dve.wait_ge(setup_pool, 1)
                    return dve.tensor_copy(dT_rep[:].rearrange("p (t b) -> p t b", b=BATCH),
                                           dT[:].rearrange("p (o b) -> p o b", o=1).broadcast_to([P, STEPS_PER_TILE, BATCH]))
                dve.wait_ge(setup_pe, 2)
                dve.wait_ge(down_in, 32)
                dve.tensor_scalar(b2e_sb[:], b2e_sb[:], 2.0, None, ALU.mult).then_inc(b2_doubled, 1)
                return dve.tensor_copy(demod[:], y_ps[:, 0:P])

            def select_stage(d, n, values, width, k, sel):
                v = values[:, 0:n, 0:width]
                least = top8[:, 0:n, k - 1:k].broadcast_to([P, n, width])
                gt, eq, bf, ft = (m[:, 0:n, 0:width] for m in (above, equal, before, fits))
                if d == 0:
                    for i in range(n):
                        ins = dve.max(top8[:, i, :], values[:, i, :])
                elif d == 1:
                    dve.tensor_tensor(gt, v, least, ALU.is_gt)
                    ins = dve.tensor_tensor(eq, v, least, ALU.is_equal)
                elif d == 2:
                    ins = dve.tensor_reduce(n_above[:, 0:n], gt, AX_X, ALU.add)
                elif d == 3:
                    for i in range(n):
                        ins = dve.tensor_tensor_scan(before[:, i, 0:width], equal[:, i, 0:width], zeros16[:, 0:width],
                                                     n_above[:, i:i + 1], ALU.add, ALU.add)
                elif d == 4:
                    ins = dve.scalar_tensor_tensor(out=ft, in0=bf, scalar=float(k), in1=eq, op0=ALU.is_le, op1=ALU.mult)
                else:
                    ins = dve.tensor_tensor(sel, ft, gt, ALU.add)
                return ins

            def gate_stage(c, d):
                first, n = CHUNKS[c]
                s, m = s_gate[:, 0:n, :], masked[:, 0:n, :]
                by_group = lambda ap: ap.rearrange("p n (g e) -> p (n g) e", g=GROUPS)
                g = g_sel[:, 0:n, :].rearrange("p n (g o) -> p (n g) o", o=1).broadcast_to([P, n * GROUPS, EXPERTS // GROUPS])
                if d == 0:
                    dve.wait_ge(exp_ready, (first + n) * EXP_PARTS)
                    return dve.tensor_scalar(s, exp_neg[:, first:first + n, :], 1.0, None, ALU.add)
                if d == 1:
                    return dve.reciprocal(s, s)
                if d == 2:
                    return dve.tensor_reduce(gmax[:, 0:n, 0:GROUPS], s.rearrange("p n (g e) -> p n g e", g=GROUPS), AX_X, ALU.max)
                if d < 9:
                    return select_stage(d - 3, n, gmax, GROUPS, TOP_GROUPS, g_sel[:, 0:n, :])
                if d == 9:
                    return dve.tensor_tensor(by_group(m), by_group(s), g, ALU.mult)
                if d == 10:
                    return dve.scalar_tensor_tensor(out=by_group(m), in0=g, scalar=-1.0, in1=by_group(m),
                                                    op0=ALU.add, op1=ALU.add)
                if d < 17:
                    return select_stage(d - 11, n, masked, EXPERTS, TOP_EXPERTS, e_sel[:, 0:n, :])
                if d == 17:
                    return dve.tensor_tensor(w_raw[:, 0:n, :], e_sel[:, 0:n, :], s, ALU.mult)
                if d == 18:
                    return dve.tensor_reduce(w_sum[:, 0:n], w_raw[:, 0:n, :], AX_X, ALU.add)
                if d == 19:
                    return dve.reciprocal(w_inv[:, 0:n], w_sum[:, 0:n])
                return dve.scalar_tensor_tensor(out=we[:, first:first + n, :], in0=w_raw[:, 0:n, :], scalar=ROUTE_SCALE / 2,
                                                in1=w_inv[:, 0:n].rearrange("p (n o) -> p n o", o=1).broadcast_to([P, n, EXPERTS]),
                                                op0=ALU.mult, op1=ALU.mult)

            marks = {}

            def mark(ins, key):
                links[0] += 1
                ins.then_inc(chain, 1)
                marks[key] = links[0]

            def after(key):
                dve.wait_ge(chain, marks[key])

            for kind, n in SCHEDULE:
                if kind == "SETUP":
                    if n:
                        dve.wait_ge(setup_dve, n)
                    setup_stage(n).then_inc(setup_dve, 1)
                if kind == "SCORES_READ":
                    wait_filled(dve, "SCORES", n)
                    dve.tensor_scalar(neg_scores[:, n, :], m_ps[:, 0:EXPERTS], -1.0, None, ALU.mult).then_inc(freed[M], 1)
                if kind == "SPLIT":
                    cols = chunk_cols(n)
                    dve.wait_ge(h_ready, (CHUNKS[n][0] + CHUNKS[n][1]) * STEPS_PER_TILE)
                    link(dve.tensor_copy(hs_hi[:, cols], hs[:, cols]))
                    dve.tensor_tensor(hs_lo[:, cols], hs[:, cols], hs_hi[:, cols].bitcast(F32), ALU.subtract).then_inc(hs_split, 1)
                if kind == "GATE":
                    c, d = divmod(n, GATE_STAGES)
                    if n:
                        dve.wait_ge(gate_step, n)
                    gate_stage(c, d).then_inc(gate_step, 1)
                if kind == "WT_READ":
                    wait_filled(dve, "WT", n)
                    dve.tensor_copy(weT[:, tile_cols(n)], m_ps[0:EXPERTS, 0:P]).then_inc(freed[M], 1)
                if kind == "GATED":
                    w = chunk_of(n)[1] * P
                    if n >= H_RING:
                        dve.wait_ge(y_done, n - H_RING + 1)
                    dve.wait_ge(gate_ready, n + 1)
                    dve.scalar_tensor_tensor(out=hid[:, n % H_RING, 0:w], in0=gate_t[:, n % 4, 0:w], scalar=1.0,
                                             in1=gate_a[:, n % 4, 0:w], op0=ALU.add, op1=ALU.mult).then_inc(gated, 1)
                if kind == "HIDDEN":
                    e = n % EXPERTS
                    w = chunk_of(n)[1] * P
                    h = hid[:, n % H_RING, 0:w]
                    dve.wait_ge(gated, n + 1)
                    dve.wait_ge(b_ready, n + 1)
                    dve.scalar_tensor_tensor(out=h, in0=b_ps[n % 2][:, 0:w], scalar=b3_sb[:, e:e + 1],
                                             in1=h, op0=ALU.add, op1=ALU.mult).then_inc(hid_ready, 1)
                if kind == "FIN_READ":
                    cols = chunk_cols(n)
                    w = CHUNKS[n][1] * P
                    if n == 0:
                        dve.wait_ge(x_in, 16)
                        dve.wait_ge(xw_in, 48)
                    dve.wait_ge(chunk_y, n + 1)
                    link(dve.tensor_tensor(x1T[:, cols], y_ps[:, 0:w], xT_sb[:, cols], ALU.add))
                    dve.tensor_tensor(zT[:, cols].rearrange("p (t b) -> p t b", b=BATCH),
                                      x1T[:, cols].rearrange("p (t b) -> p t b", b=BATCH),
                                      ysT[:].rearrange("p (o b) -> p o b", o=1).broadcast_to([P, w // BATCH, BATCH]),
                                      ALU.mult).then_inc(x1_ready, 1)
                if kind == "X_READ":
                    bank = banks[bank_of("X", n)]
                    wait_filled(dve, "X", n)
                    dve.tensor_tensor(x1b[:, n, :], bank[:, 0:P], fb2_bc[:], ALU.add)
                    dve.tensor_tensor(o_sb[:, n % 2, :], bank[:, P:2 * P], demod[:], ALU.mult).then_inc(freed[bank_of("X", n)], 1)
                which = 0 if kind.endswith("1") else 1
                one = slice(2 * n + which, 2 * n + which + 1)
                if kind == "AMAX1":
                    wait_read(dve, "X", n)
                    mark(dve.tensor_reduce(amax[:, one], o_sb[:, n % 2, :], AX_X, ALU.max, apply_absolute_value=True), (kind, n))
                if kind == "AMAX2":
                    dve.wait_ge(gelu_ready, n + 1)
                    mark(dve.tensor_reduce(amax[:, one], hp[:, n % 4, :], AX_X, ALU.max, apply_absolute_value=True), (kind, n))
                if kind in ("SCALE1", "SCALE2"):
                    after((f"AMAX{which + 1}", n))
                    mark(dve.tensor_scalar(step[:, one], amax[:, one], 1e-5, 1.0 / QB, ALU.max, ALU.mult), (kind, n))
                if kind in ("RECIP1", "RECIP2"):
                    after((f"SCALE{which + 1}", n))
                    dve.tensor_scalar(deq[:, one], step[:, one], f_scale[:, which:which + 1], None, ALU.mult)
                    ins = dve.reciprocal(inv_step[:, one], step[:, one])
                    if kind == "RECIP2" and n >= ROUND_ACT_FROM:
                        ins.then_inc(inv_ready, 1)
                    else:
                        mark(ins, (kind, n))
                if kind == "ROUND1":
                    after(("RECIP1", n))
                    mark(dve.tensor_scalar(q_f[:, n % 2, :], o_sb[:, n % 2, :], inv_step[:, one], MAGIC, ALU.mult, ALU.add), (kind, n))
                if kind == "ROUND2" and n < ROUND_ACT_FROM:
                    after(("RECIP2", n))
                    mark(dve.tensor_scalar(q2_f[:, n % 2, :], hp[:, n % 4, :], inv_step[:, one], MAGIC, ALU.mult, ALU.add), (kind, n))
                if kind == "INT1":
                    after(("ROUND1", n))
                    dve.tensor_scalar(q_bf[:, n % 2, :], q_f[:, n % 2, :], MAGIC, QB, ALU.subtract, ALU.min).then_inc(q_ready, 1)
                if kind == "INT2":
                    if n < ROUND_ACT_FROM:
                        after(("ROUND2", n))
                    else:
                        dve.wait_ge(act_rounded, n - ROUND_ACT_FROM + 1)
                    dve.tensor_scalar(q2_bf[:, n % 2, :], q2_f[:, n % 2, :], MAGIC, QB, ALU.subtract, ALU.min).then_inc(q2_ready, 1)
                if kind == "Q_READ":
                    wait_filled(dve, "Q", n)
                    dve.tensor_copy(qT[:, n % 2, :], m_ps[:, 0:P // 2].bitcast(BF16)).then_inc(freed[M], 1)
                if kind == "HP_READ":
                    wait_filled(dve, "HP", n)
                    b = bank_of("HP", n)
                    dve.scalar_tensor_tensor(out=hp[:, n % 4, :], in0=banks[b][:], scalar=deq[:, 2 * n:2 * n + 1],
                                             in1=fb1_bc[:], op0=ALU.mult, op1=ALU.add).then_inc(freed[b], 1)
                if kind == "OUT_READ":
                    b = bank_of("OUT", n)
                    wait_filled(dve, "OUT", n)
                    dve.scalar_tensor_tensor(out=out_sb[:, n, :], in0=banks[b][:, 0:P], scalar=deq[:, 2 * n + 1:2 * n + 2],
                                             in1=x1b[:, n, :], op0=ALU.mult, op1=ALU.add).then_inc(freed[b], 1)

        @block.tensor
        def _(pe):
            def rnn_inputs(i):
                ps = rnn_bank(i * P, P)
                pe.matmul(ps, wx_sb[:], xT_sb[:, tile_cols(i)], start=(i in (0, 1, BANK // P)), stop=False,
                          skip_group_check=True)
                pe.matmul(ps, bh_sb[:], ones_row[:, 0:P], start=False, stop=False, skip_group_check=True)

            def product(ps, w32, hi, lo, j, p, ready):
                c, e = divmod(j, EXPERTS)
                cols, ex = chunk_cols(c), expert_cols(e)
                w = CHUNKS[c][1] * P
                single = CHUNKS[c][1] == 1
                left, right = (w32, hs) if single else ((lo, hs_hi), (hi, hs_lo), (hi, hs_hi))[p]
                last = single or p == 2
                ins = pe.matmul(ps[:, 0:w], left[:, ex], right[:, cols], start=(p == 0), stop=last)
                if last:
                    ins.then_inc(ready, 1)

            def keep_warm(j):
                if j >= 2:
                    pe.wait_ge(gate_ready, j - 1)
                pe.matmul(a_ps[j % 2][:, 0:256], warm_sb[:, 0:P], warm_sb[:], start=True, stop=True)

            pe.wait_ge(warm_ready, 1)
            for _ in range(START_KEEPS):
                keep_warm(0)
            pe.wait_ge(xw_in, 48)
            pe.wait_ge(ones_ready, 1)
            rnn_inputs(0)
            for kind, n in SCHEDULE:
                if kind == "RNN":
                    if n == 0:
                        pe.wait_ge(rnn_in, 32)
                    else:
                        pe.wait_ge(h_ready, n)
                    prev = h0_sb[:] if n == 0 else hs[:, (n - 1) * BATCH:n * BATCH]
                    pe.matmul(rnn_bank(n * BATCH, BATCH), wh_sb[:], prev, start=False, stop=True,
                              skip_group_check=True).then_inc(z_ready, 1)
                    if n == 2:
                        pe.wait_ge(x_in, 16)
                    if 2 <= n <= TILES:
                        rnn_inputs(n - 1)
                if (kind, n) == ("SETUP", 2):
                    pe.wait_ge(ones_sq_ready, 1)
                    pe.wait_ge(setup_dve, 3)
                    pe.matmul(y_ps[:, 0:BATCH], wc2[:], ys2[:], start=True, stop=True, skip_group_check=True)
                    pe.matmul(y_ps[:, BATCH:BATCH + 2], ones_sq[:], f_abs[:], start=True, stop=True,
                              skip_group_check=True).then_inc(setup_pe, 1)
                if (kind, n) == ("SETUP", 8):
                    pe.wait_ge(setup_dve, 9)
                    pe.transpose(y_ps[:, 0:P], dT_rep[:], ident[:]).then_inc(setup_pe, 1)
                if kind == "SCORES":
                    if n == 0:
                        pe.wait_ge(gate_in, 16)
                    if n == TILES - 1:
                        pe.wait_ge(h_ready, STEPS)
                    wait_free(pe, kind, n)
                    pe.matmul(m_ps[:, 0:EXPERTS], hs[:, tile_cols(n)], wg_sb[:], start=True, stop=True).then_inc(filled[M], 1)
                if kind == "WT":
                    c = chunk_with(n)
                    pe.wait_ge(gate_step, (c + 1) * GATE_STAGES)
                    wait_free(pe, kind, n)
                    pe.transpose(m_ps[0:EXPERTS, 0:P], we[:, n, :], ident[:]).then_inc(filled[M], 1)
                if kind == "KEEP":
                    keep_warm(n)
                if kind in ("A", "B"):
                    j, p = divmod(n, MAX_PASSES)
                    c = j // EXPERTS
                if kind == "A":
                    if p == 0:
                        if j == 0:
                            pe.wait_ge(moe_in, 32)
                        if CHUNKS[c][1] > 1:
                            first_big = min(k for k, ch in enumerate(CHUNKS) if ch[1] > 1)
                            pe.wait_ge(w1_split, EXPERTS * P // BANK)
                            pe.wait_ge(w3_split, EXPERTS * P // BANK)
                            pe.wait_ge(hs_split, c - first_big + 1)
                        if j >= 2:
                            pe.wait_ge(gate_ready, j - 1)
                    product(a_ps[j % 2], w1_sb, w1_hi, w1_lo, j, p, a_ready)
                if kind == "B":
                    if p == 0 and j >= 2:
                        pe.wait_ge(hid_ready, j - 1)
                    product(b_ps[j % 2], w3_sb, w3_hi, w3_lo, j, p, b_ready)
                if kind == "Y":
                    j, p = divmod(n, 2)
                    c, e = divmod(j, EXPERTS)
                    tiles = CHUNKS[c][1]
                    if n == 0:
                        pe.wait_ge(setup_dve, SETUP_STAGES)
                        pe.wait_ge(down_in, 32)
                    if e == 0 and p == 0 and c:
                        pe.wait_ge(x1_ready, c)
                    pe.wait_ge(hid_weighted, j + 1)
                    ins = pe.matmul(y_ps[:, tile_cols(p)], w2_sb[:, expert_cols(e)], hid[:, j % H_RING, tile_cols(p)],
                                    start=(e == 0 and p == 0), stop=False, skip_group_check=True)
                    if p == tiles - 1:
                        ins.then_inc(y_done, 1)
                if kind == "FIN":
                    pe.wait_ge(b2_doubled, 1)
                    wait_read(pe, "WT", CHUNKS[n][0] + CHUNKS[n][1] - 1)
                    pe.matmul(y_ps[:, 0:CHUNKS[n][1] * P], b2e_sb[:], weT[:, chunk_cols(n)],
                              start=False, stop=True, skip_group_check=True).then_inc(chunk_y, 1)
                if kind == "X":
                    bank = banks[bank_of(kind, n)]
                    c = chunk_with(n)
                    pe.wait_ge(x1_ready, c + 1)
                    wait_free(pe, kind, n)
                    pe.transpose(bank[:, 0:P], x1T[:, tile_cols(n)], ident[:])
                    pe.matmul(bank[:, P:2 * P], zT[:, tile_cols(n)], wc_sb[:], start=True, stop=True,
                              skip_group_check=True).then_inc(filled[bank_of(kind, n)], 1)
                if kind == "Q":
                    pe.wait_ge(q_ready, n + 1)
                    wait_free(pe, kind, n)
                    pe.transpose(m_ps[:, 0:P // 2].bitcast(BF16), q_bf[:, n % 2, :], ident_bf[:]).then_inc(filled[M], 1)
                if kind == "HP":
                    b = bank_of(kind, n)
                    wait_read(pe, "Q", n)
                    wait_free(pe, kind, n)
                    pe.matmul(banks[b][:], qT[:, n % 2, :], f1_q[:], start=True, stop=True).then_inc(filled[b], 1)
                if kind == "T2":
                    b = bank_of(kind, n)
                    pe.wait_ge(q2_ready, n + 1)
                    wait_free(pe, kind, n)
                    for k in range(HB):
                        last = pe.transpose(banks[b][:, k * P // 2:(k + 1) * P // 2].bitcast(BF16),
                                            q2_bf[:, n % 2, k * P:(k + 1) * P], ident_bf[:])
                    last.then_inc(filled[b], 1)
                if kind == "OUT":
                    b = bank_of(kind, n)
                    wait_read(pe, "T2", n)
                    wait_free(pe, kind, n)
                    for k in range(HB):
                        last = pe.matmul(banks[b][:, 0:P], q2T[:, n % 2, k * P:(k + 1) * P], f2_q[:, k, :],
                                         start=(k == 0), stop=(k == HB - 1))
                    last.then_inc(filled[b], 1)


def kernel(x, cond_1024, L0_cond_Wx, L0_cond_Wh, L0_cond_b, L0_ffn_Wg, L0_ffn_W1, L0_ffn_b1,
           L0_ffn_W2, L0_ffn_b2, L0_ffn_W3, L0_ffn_b3, L1_cond_weight, L1_ffn_W1, L1_ffn_b1,
           L1_ffn_W2, L1_ffn_b2):
    import numpy as np
    import concourse.bacc as bacc
    from concourse.bass_utils import run_bass_kernel_spmd

    def lay(a, *shape):
        return np.ascontiguousarray(a).reshape(shape)

    x = np.asarray(x)
    by_step = x.transpose(1, 0, 2).reshape(TOKENS, P)
    cond = np.asarray(cond_1024)
    experts = lambda w: lay(np.asarray(w).transpose(2, 0, 1), P, EXPERTS * P)
    arrays = {
        "xT": lay(by_step.T, P, TOKENS),
        "h0T": lay(cond.T, P, BATCH),
        "Wx": lay(L0_cond_Wx, P, P),
        "Wh": lay(L0_cond_Wh, P, P),
        "bh": lay(L0_cond_b, 1, P),
        "WgT": lay(np.asarray(L0_ffn_Wg).T, P, EXPERTS),
        "W1T": experts(L0_ffn_W1),
        "W3T": experts(L0_ffn_W3),
        "W2T": experts(L0_ffn_W2),
        "b1T": lay(np.asarray(L0_ffn_b1).T, P, EXPERTS),
        "b3T": lay(np.asarray(L0_ffn_b3).T, P, EXPERTS),
        "b2e": lay(L0_ffn_b2, EXPERTS, P),
        "condT": lay(cond.T, P, BATCH),
        "Wc": lay(L1_cond_weight, P, P),
        "F1T": lay(np.asarray(L1_ffn_W1).T, P, HIDDEN),
        "F2T": lay(np.asarray(L1_ffn_W2).T.reshape(HB, P, P).transpose(1, 0, 2), P, HIDDEN),
        "fb1": lay(L1_ffn_b1, 1, HIDDEN),
        "fb2": lay(L1_ffn_b2, 1, P),
    }
    nc = bacc.Bacc("TRN2", target_bir_lowering=False, num_devices=1)
    aps = {name: nc.dram_tensor(name, a.shape, F32, kind="ExternalInput").ap() for name, a in arrays.items()}
    we_dram = nc.dram_tensor("we_dram", (EXPERTS, TOKENS), F32, kind="Internal").ap()
    out = nc.dram_tensor("out", (TILES, P, P), F32, kind="ExternalOutput").ap()
    adaln_ffn(nc, we_dram=we_dram, out=out, **aps)
    r = run_bass_kernel_spmd(nc, [arrays], core_ids=[0])
    y = r.results[0]["out"]
    return np.ascontiguousarray(y.reshape(STEPS, BATCH, P).transpose(1, 0, 2))
```
